# Optimizing a Trainium2 kernel written in Bass

```python
import numpy as np
import jax
import jax.numpy as jnp

def _softmax(x, axis=-1):
    return jax.nn.softmax(x, axis=axis)

def _gelu(x):
    return jax.nn.gelu(x, approximate=True)

def _silu(x):
    return jax.nn.silu(x)

def _sigmoid(x):
    return jax.nn.sigmoid(x)

def _layernorm(x, axis=-1, eps=1e-05):
    m = jnp.mean(x, axis=axis, keepdims=True)
    v = jnp.var(x, axis=axis, keepdims=True)
    return (x - m) / jnp.sqrt(v + eps)

def _scatter_add(tgt, idx, src, axis=0):
    return tgt.at[idx].add(src)

def _segment_sum(src, seg, n):
    return jax.ops.segment_sum(src, seg, n)
kernel_name = 'mk_decoder_postln_d1_seqx_r4_299f48'

def setup_inputs(seed: int=0):
    np.random.seed(seed)
    _w = jnp.asarray

    def _rec_inputs():
        import jax
        import jax.numpy as jnp
        _rk = jax.random.key(seed)
        x = -9.806e-05 + 1 * jax.random.normal(jax.random.fold_in(_rk, 1), (8, 512, 256), jnp.float32)
        _lenS = 512 - jax.random.randint(jax.random.fold_in(_rk, 7), (8,), 0, max(1, 512 // 4) + 1, jnp.int32)
        _lenS2 = 64 - jax.random.randint(jax.random.fold_in(_rk, 8), (8,), 0, max(1, 64 // 4) + 1, jnp.int32)
        _ctx_1024P = jax.random.normal(jax.random.fold_in(_rk, 11), (8, 16, 256), jnp.float32)
        _ctx_1024c = jax.random.dirichlet(jax.random.fold_in(_rk, 511), 0.3 * jnp.ones((16,), jnp.float32), (8, 64))
        _ctx_1024t = jnp.einsum('bsk,bkd->bsd', _ctx_1024c, _ctx_1024P)
        _ctx_1024t = _ctx_1024t * jax.lax.rsqrt(jnp.mean(jnp.square(_ctx_1024t)) + 1e-12) * 0.953939
        ctx_1024 = -1.52775e-05 + 0.999936 * (_ctx_1024t + 0.3 * jax.random.normal(jax.random.fold_in(_rk, 611), (8, 64, 256), jnp.float32))
        return (x, ctx_1024)
    x, ctx_1024 = _rec_inputs()

    def _L0_attn_setup():
        import jax, jax.numpy as jnp
        import numpy as np
        B_, L_, E_ = (2, 512, 256)
        EXPAND, DSTATE, DCONV = (2, 16, 4)
        DIN = EXPAND * E_
        DTR = E_ // 16

        def _layer_norm(x, g, b, eps=1e-05):
            mu = jnp.mean(x, axis=-1, keepdims=True)
            var = jnp.mean(jnp.square(x - mu), axis=-1, keepdims=True)
            return (x - mu) * jax.lax.rsqrt(var + eps) * g + b

        def _mamba_forward(x, ln_g, ln_b, W_in, conv_w, conv_b, W_x, W_dt, dt_bias, A_log, D, W_out):
            L = x.shape[1]
            xn = _layer_norm(x, ln_g, ln_b)
            xz = jnp.einsum('ble,de->bld', xn, W_in)
            u, z = (xz[..., :DIN], xz[..., DIN:])
            up = jnp.pad(u, ((0, 0), (DCONV - 1, 0), (0, 0)))
            uc = conv_b
            uc = sum((conv_w[:, k] * up[:, k:k + L, :] for k in range(DCONV))) + conv_b
            u = jax.nn.silu(uc)
            dbc = jnp.einsum('bld,rd->blr', u, W_x)
            dt_in = dbc[..., :DTR]
            Bm = dbc[..., DTR:DTR + DSTATE]
            Cm = dbc[..., DTR + DSTATE:]
            dt = jax.nn.softplus(jnp.einsum('blr,dr->bld', dt_in, W_dt) + dt_bias)
            A = -jnp.exp(A_log)
            dA = jnp.exp(dt[..., None] * A)
            dBu = dt[..., None] * Bm[:, :, None, :] * u[..., None]

            def step(h, e):
                da, dbu, c = e
                h = da * h + dbu
                y = jnp.einsum('bdn,bn->bd', h, c)
                return (h, y)
            elems = (jnp.moveaxis(dA, 1, 0), jnp.moveaxis(dBu, 1, 0), jnp.moveaxis(Cm, 1, 0))
            h0 = jnp.zeros((x.shape[0], DIN, DSTATE), x.dtype)
            _, ys = jax.lax.scan(step, h0, elems)
            y = jnp.moveaxis(ys, 0, 1) + u * D
            y = y * jax.nn.silu(z)
            out = jnp.einsum('bld,ed->ble', y, W_out)
            return x + out
        key = jax.random.key(seed)
        ks = jax.random.split(key, 8)
        s = 0.02
        f32 = jnp.float32
        A_log = jnp.tile(jnp.log(jnp.arange(1, DSTATE + 1, dtype=f32)), (DIN, 1))
        return {'x': jax.random.normal(ks[0], (B_, L_, E_), f32), 'ln_g': jnp.ones((E_,), f32), 'ln_b': jnp.zeros((E_,), f32), 'W_in': jax.random.normal(ks[1], (2 * DIN, E_), f32) * s, 'conv_w': jax.random.normal(ks[2], (DIN, DCONV), f32) * s, 'conv_b': jnp.zeros((DIN,), f32), 'W_x': jax.random.normal(ks[3], (DTR + 2 * DSTATE, DIN), f32) * s, 'W_dt': jax.random.normal(ks[4], (DIN, DTR), f32) * s, 'dt_bias': jax.random.normal(ks[5], (DIN,), f32) * 0.01, 'A_log': A_log, 'D': jnp.ones((DIN,), f32), 'W_out': jax.random.normal(ks[6], (E_, DIN), f32) * s}
    _L0_attn_all = _L0_attn_setup()
    _L0_attn_in = {k: v for k, v in _L0_attn_all.items() if k in ('ln_g', 'ln_b', 'W_in', 'conv_w', 'conv_b', 'W_x', 'W_dt', 'dt_bias', 'A_log', 'D', 'W_out')}
    del _L0_attn_all

    def _L0_xattn_setup():
        import jax, jax.numpy as jnp
        import numpy as np
        D = 256
        NUM_ITERS = 3
        EPS = 1e-06
        SCALE = D ** (-0.5)

        def rmsnorm(x, w, eps=EPS):
            return x * jax.lax.rsqrt(jnp.mean(x * x, axis=-1, keepdims=True) + eps) * w

        def gru_cell(x, h, wih, whh, bih, bhh):
            gx = x @ wih.T + bih
            gh = h @ whh.T + bhh
            xr, xz, xn = jnp.split(gx, 3, axis=-1)
            hr, hz, hn = jnp.split(gh, 3, axis=-1)
            r = jax.nn.sigmoid(xr + hr)
            z = jax.nn.sigmoid(xz + hz)
            n = jnp.tanh(xn + r * hn)
            return (1.0 - z) * n + z * h
        key = jax.random.key(seed)
        ks = jax.random.split(key, 8)
        B, K, M, d = (8, 64, 1024, D)
        w_std = d ** (-0.5)
        return {'slots': jax.random.normal(ks[0], (B, K, d), jnp.float32), 'P': jax.random.normal(ks[1], (B, M, d), jnp.float32), 'Wq': jax.random.normal(ks[2], (d, d), jnp.float32) * w_std, 'Wk': jax.random.normal(ks[3], (d, d), jnp.float32) * w_std, 'Wv': jax.random.normal(ks[4], (d, d), jnp.float32) * w_std, 'gru_wih': jax.random.normal(ks[5], (3 * d, d), jnp.float32) * w_std, 'gru_whh': jax.random.normal(ks[6], (3 * d, d), jnp.float32) * w_std, 'gru_bih': jnp.zeros((3 * d,), jnp.float32), 'gru_bhh': jnp.zeros((3 * d,), jnp.float32), 'slot_norm_w': jnp.ones((d,), jnp.float32), 'input_norm_w': jnp.ones((d,), jnp.float32)}
    _L0_xattn_all = _L0_xattn_setup()
    _L0_xattn_in = {k: v for k, v in _L0_xattn_all.items() if k in ('Wq', 'Wk', 'Wv', 'gru_wih', 'gru_whh', 'gru_bih', 'gru_bhh', 'slot_norm_w', 'input_norm_w')}
    del _L0_xattn_all

    def _L0_ffn_setup():
        import jax, jax.numpy as jnp
        import numpy as np
        import math
        BETA = 0.9
        THRESHOLD = 1.0
        NUM_STEPS = 5
        ALPHA = 2.0

        @jax.custom_vjp
        def spike_fn(u):
            return (u > 0).astype(u.dtype)

        def _spike_fwd(u):
            return (spike_fn(u), u)

        def _spike_bwd(u, g):
            s = jnp.pi / 2.0 * ALPHA * u
            return (g * (ALPHA / 2.0) / (1.0 + s * s),)
        spike_fn.defvjp(_spike_fwd, _spike_bwd)
        key = jax.random.key(seed)
        k1, k2, k3 = jax.random.split(key, 3)
        n_embd = 256
        x = jax.random.normal(k1, (4, 512, n_embd), dtype=jnp.float32)
        W_fc = jax.random.normal(k2, (4 * n_embd, n_embd), dtype=jnp.float32) / math.sqrt(n_embd)
        W_proj = jax.random.normal(k3, (n_embd, 4 * n_embd), dtype=jnp.float32) / math.sqrt(4 * n_embd)
        return {'x': x, 'W_fc': W_fc, 'W_proj': W_proj}
    _L0_ffn_all = _L0_ffn_setup()
    _L0_ffn_in = {k: v for k, v in _L0_ffn_all.items() if k in ('W_fc', 'W_proj')}
    del _L0_ffn_all
    return {'x': x, 'ctx_1024': ctx_1024, 'L0_attn_ln_g': _L0_attn_in['ln_g'], 'L0_attn_ln_b': _L0_attn_in['ln_b'], 'L0_attn_W_in': _L0_attn_in['W_in'], 'L0_attn_conv_w': _L0_attn_in['conv_w'], 'L0_attn_conv_b': _L0_attn_in['conv_b'], 'L0_attn_W_x': _L0_attn_in['W_x'], 'L0_attn_W_dt': _L0_attn_in['W_dt'], 'L0_attn_dt_bias': _L0_attn_in['dt_bias'], 'L0_attn_A_log': _L0_attn_in['A_log'], 'L0_attn_D': _L0_attn_in['D'], 'L0_attn_W_out': _L0_attn_in['W_out'], 'L0_xattn_Wq': _L0_xattn_in['Wq'], 'L0_xattn_Wk': _L0_xattn_in['Wk'], 'L0_xattn_Wv': _L0_xattn_in['Wv'], 'L0_xattn_gru_wih': _L0_xattn_in['gru_wih'], 'L0_xattn_gru_whh': _L0_xattn_in['gru_whh'], 'L0_xattn_gru_bih': _L0_xattn_in['gru_bih'], 'L0_xattn_gru_bhh': _L0_xattn_in['gru_bhh'], 'L0_xattn_slot_norm_w': _L0_xattn_in['slot_norm_w'], 'L0_xattn_input_norm_w': _L0_xattn_in['input_norm_w'], 'L0_ffn_W_fc': _L0_ffn_in['W_fc'], 'L0_ffn_W_proj': _L0_ffn_in['W_proj']}

def reference(x, ctx_1024, L0_attn_ln_g, L0_attn_ln_b, L0_attn_W_in, L0_attn_conv_w, L0_attn_conv_b, L0_attn_W_x, L0_attn_W_dt, L0_attn_dt_bias, L0_attn_A_log, L0_attn_D, L0_attn_W_out, L0_xattn_Wq, L0_xattn_Wk, L0_xattn_Wv, L0_xattn_gru_wih, L0_xattn_gru_whh, L0_xattn_gru_bih, L0_xattn_gru_bhh, L0_xattn_slot_norm_w, L0_xattn_input_norm_w, L0_ffn_W_fc, L0_ffn_W_proj):
    import jax
    import jax.numpy as jnp

    def _L0_attn_ref(x, ln_g, ln_b, W_in, conv_w, conv_b, W_x, W_dt, dt_bias, A_log, D, W_out):
        import jax, jax.numpy as jnp
        import numpy as np
        B_, L_, E_ = (2, 512, 256)
        EXPAND, DSTATE, DCONV = (2, 16, 4)
        DIN = EXPAND * E_
        DTR = E_ // 16

        def _layer_norm(x, g, b, eps=1e-05):
            mu = jnp.mean(x, axis=-1, keepdims=True)
            var = jnp.mean(jnp.square(x - mu), axis=-1, keepdims=True)
            return (x - mu) * jax.lax.rsqrt(var + eps) * g + b

        def _mamba_forward(x, ln_g, ln_b, W_in, conv_w, conv_b, W_x, W_dt, dt_bias, A_log, D, W_out):
            L = x.shape[1]
            xn = _layer_norm(x, ln_g, ln_b)
            xz = jnp.einsum('ble,de->bld', xn, W_in)
            u, z = (xz[..., :DIN], xz[..., DIN:])
            up = jnp.pad(u, ((0, 0), (DCONV - 1, 0), (0, 0)))
            uc = conv_b
            uc = sum((conv_w[:, k] * up[:, k:k + L, :] for k in range(DCONV))) + conv_b
            u = jax.nn.silu(uc)
            dbc = jnp.einsum('bld,rd->blr', u, W_x)
            dt_in = dbc[..., :DTR]
            Bm = dbc[..., DTR:DTR + DSTATE]
            Cm = dbc[..., DTR + DSTATE:]
            dt = jax.nn.softplus(jnp.einsum('blr,dr->bld', dt_in, W_dt) + dt_bias)
            A = -jnp.exp(A_log)
            dA = jnp.exp(dt[..., None] * A)
            dBu = dt[..., None] * Bm[:, :, None, :] * u[..., None]

            def step(h, e):
                da, dbu, c = e
                h = da * h + dbu
                y = jnp.einsum('bdn,bn->bd', h, c)
                return (h, y)
            elems = (jnp.moveaxis(dA, 1, 0), jnp.moveaxis(dBu, 1, 0), jnp.moveaxis(Cm, 1, 0))
            h0 = jnp.zeros((x.shape[0], DIN, DSTATE), x.dtype)
            _, ys = jax.lax.scan(step, h0, elems)
            y = jnp.moveaxis(ys, 0, 1) + u * D
            y = y * jax.nn.silu(z)
            out = jnp.einsum('bld,ed->ble', y, W_out)
            return x + out
        return _mamba_forward(x, ln_g, ln_b, W_in, conv_w, conv_b, W_x, W_dt, dt_bias, A_log, D, W_out)

    def _L0_xattn_ref(slots, P, Wq, Wk, Wv, gru_wih, gru_whh, gru_bih, gru_bhh, slot_norm_w, input_norm_w):
        import jax, jax.numpy as jnp
        import numpy as np
        D = 256
        NUM_ITERS = 3
        EPS = 1e-06
        SCALE = D ** (-0.5)

        def rmsnorm(x, w, eps=EPS):
            return x * jax.lax.rsqrt(jnp.mean(x * x, axis=-1, keepdims=True) + eps) * w

        def gru_cell(x, h, wih, whh, bih, bhh):
            gx = x @ wih.T + bih
            gh = h @ whh.T + bhh
            xr, xz, xn = jnp.split(gx, 3, axis=-1)
            hr, hz, hn = jnp.split(gh, 3, axis=-1)
            r = jax.nn.sigmoid(xr + hr)
            z = jax.nn.sigmoid(xz + hz)
            n = jnp.tanh(xn + r * hn)
            return (1.0 - z) * n + z * h
        Pn = rmsnorm(P, input_norm_w)
        k_proj = Pn @ Wk.T
        v_proj = Pn @ Wv.T
        for _ in range(NUM_ITERS):
            sn = rmsnorm(slots, slot_norm_w)
            q_proj = sn @ Wq.T
            scores = jnp.einsum('bkd,bmd->bkm', q_proj, k_proj) * SCALE
            attn = jax.nn.softmax(scores, axis=-2)
            attn = attn / (jnp.sum(attn, axis=-1, keepdims=True) + EPS)
            updates = jnp.einsum('bkm,bmd->bkd', attn, v_proj)
            slots = gru_cell(updates, slots, gru_wih, gru_whh, gru_bih, gru_bhh)
        return slots

    def _L0_ffn_ref(x, W_fc, W_proj):
        import jax, jax.numpy as jnp
        import numpy as np
        import math
        BETA = 0.9
        THRESHOLD = 1.0
        NUM_STEPS = 5
        ALPHA = 2.0

        @jax.custom_vjp
        def spike_fn(u):
            return (u > 0).astype(u.dtype)

        def _spike_fwd(u):
            return (spike_fn(u), u)

        def _spike_bwd(u, g):
            s = jnp.pi / 2.0 * ALPHA * u
            return (g * (ALPHA / 2.0) / (1.0 + s * s),)
        spike_fn.defvjp(_spike_fwd, _spike_bwd)
        h = jnp.square(jax.nn.relu(jnp.einsum('bsd,fd->bsf', x, W_fc)))
        y = jnp.einsum('bsf,df->bsd', h, W_proj)

        def step(mem, _):
            reset = jax.lax.stop_gradient(spike_fn(mem - THRESHOLD))
            mem_new = BETA * mem + y - reset * THRESHOLD
            spk = spike_fn(mem_new - THRESHOLD)
            return (mem_new, spk)
        mem0 = jnp.zeros_like(y)
        _, spks = jax.lax.scan(step, mem0, None, length=NUM_STEPS)
        return jnp.sum(spks, axis=0) / NUM_STEPS
    x = _layernorm(x + _L0_attn_ref(x, L0_attn_ln_g, L0_attn_ln_b, L0_attn_W_in, L0_attn_conv_w, L0_attn_conv_b, L0_attn_W_x, L0_attn_W_dt, L0_attn_dt_bias, L0_attn_A_log, L0_attn_D, L0_attn_W_out), axis=-1)
    x = _layernorm(x + _L0_xattn_ref(x, ctx_1024, L0_xattn_Wq, L0_xattn_Wk, L0_xattn_Wv, L0_xattn_gru_wih, L0_xattn_gru_whh, L0_xattn_gru_bih, L0_xattn_gru_bhh, L0_xattn_slot_norm_w, L0_xattn_input_norm_w), axis=-1)
    x = _layernorm(x + _L0_ffn_ref(x, L0_ffn_W_fc, L0_ffn_W_proj), axis=-1)
    return x

_drawn_inputs = setup_inputs


def setup_inputs(seed=0):
    import zlib

    import numpy as np

    out = dict(_drawn_inputs(seed))
    spreads = {'L0_attn_ln_g': (1.0, 0.6),
     'L0_attn_ln_b': (0.0, 0.8),
     'L0_attn_conv_b': (0.0, 0.8),
     'L0_attn_D': (1.0, 0.6),
     'L0_xattn_gru_bih': (0.0, 0.1),
     'L0_xattn_gru_bhh': (0.0, 0.1),
     'L0_xattn_slot_norm_w': (1.0, 0.2),
     'L0_xattn_input_norm_w': (1.0, 0.2)}
    factors = {'L0_attn_W_in': 7.125,
     'L0_attn_conv_w': 8.0,
     'L0_attn_W_x': 8.0,
     'L0_attn_W_dt': 8.0,
     'L0_attn_dt_bias': 8.0,
     'L0_attn_A_log': 8.0,
     'L0_attn_W_out': 6.903}
    for name, (base, spread) in spreads.items():
        noise = np.random.default_rng([zlib.crc32(name.encode()), seed]).standard_normal(out[name].shape)
        drawn = base * np.exp(spread * noise) if base else spread * noise
        out[name] = jnp.asarray(drawn.astype(out[name].dtype))
    for name, factor in factors.items():
        out[name] = (out[name] * factor).astype(out[name].dtype)
    return out
```

```python
from contextlib import ExitStack

import concourse.bass as bass
from concourse import mybir

F32 = mybir.dt.float32
BF16 = mybir.dt.bfloat16
ALU = mybir.AluOpType
ACT = mybir.ActivationFunctionType
AX = mybir.AxisListType

P = 128
BATCH, L, E = 8, 512, 256
DIN, NS, DTR, KC = 512, 16, 16, 4
M = 64
F = 4 * E
NI = 3
ET, DT, FT, TT = E // P, DIN // P, F // P, L // P
BC = 2 * NS
PAIRS = NS // 2
GROUPS = DT * PAIRS
LAG = 2
SCALE = float(E) ** -0.5
LN_EPS, RMS_EPS = 1e-5, 1e-6
BETA, THRESHOLD, STEPS = 0.9, 1.0, 5
HR = 3

COLS = {}
_at = 0
for _name, _n in (("conv_w", DT * KC), ("conv_b", DT), ("dt_bias", DT), ("A_log", DT * NS), ("D", DT),
                  ("bih", 6), ("bhh", 6), ("slot_w", ET), ("input_w", ET), ("ln_g", ET), ("ln_b", ET)):
    COLS[_name] = slice(_at, _at + _n)
    _at += _n
NCOLS = _at

COUNTS = """
pre_stat pre_aggr pre_ve pre_rs pre_norm pre_full xnT_ready upad_zero uacc_ready conv_step uth_ready u_ready
zth_ready sz_ready bc_split dtin_ready sp_abs sp_exp sp_ln dt_ready dtu_ready da_zero
cb_full cb_ready bcb_full da_ready mul_done scan_done hc_done hsum_done ypost_done yz_done
op_full res_done post_stat post_aggr post_ve post_rs post_norm post_full hT_loaded
c_sq c_ve c_rs c_norm x_full pnT_ready g_ready vw_ready sq_ready lnss_done rsb_done sc_done mx_done nmx_done ex_done
rz_done an0_done eps_done rt_done an_done trz_ready nh_ready v1_done v2_done n_ready d_done e_done h_done
xs_done x2_stat x2_aggr x2_ve x2_rs x2_norm x2T_ready
f_full f_relu f_sq y_copied spike out_res out_stat out_aggr out_ve out_rs out_norm
xin_load xres_load ctx_load out_store
""".split()


def decoder_layer(nc, x, ctx_in, cols_d, w_inT, w_xT, w_dtT, w_outT, wq_d, wk_d, wv_d, wihT, whhT, w_fcT, w_prT, out):
    with ExitStack() as ctx:
        def sb(name, shape, dt=F32):
            return ctx.enter_context(nc.sbuf_tensor(name, shape, dt))

        def ps(name, shape):
            return ctx.enter_context(nc.psum_tensor(name, shape, F32))

        w_in = sb("w_in", [P, ET, 2 * DIN])
        w_x = sb("w_x", [P, DT, DTR + 3 * BC])
        w_dt = sb("w_dt", [DTR, DIN])
        w_out = sb("w_out", [P, DT, E])
        whh = sb("whh", [P, ET, 3 * E])
        wvih = sb("wvih", [P, ET, 3 * E])
        mqk = sb("mqk", [P, ET, E])
        w_fc = sb("w_fc", [P, ET, F])
        w_pr = sb("w_pr", [P, FT, E])
        cols = sb("cols", [P, NCOLS])
        neg_a = sb("neg_a", [P, DT * NS])
        half_b = sb("half_b", [P, 6])
        half_d = sb("half_d", [P, DT])
        g_scale = sb("g_scale", [P, ET])
        ident = sb("ident", [P, P])
        ones = sb("ones", [P, M])
        mhalf = sb("mhalf", [P, TT])
        rms_eps = sb("rms_eps", [P, 1])
        sel32 = sb("sel32", [3 * BC, BC])
        sel = sb("sel", [3 * BC, BC, P], BF16)

        reg_a = sb("reg_a", [P, 2060 + HR * 1024])
        reg_c = sb("reg_c", [P, NS, L])
        reg_y = sb("reg_y", [P, DT, L])
        upad = reg_a[:, 0:2060].rearrange("p (c t) -> p c t", c=DT)
        d_a = reg_a[:, 0:2048].rearrange("p (s n t) -> p s n t", s=2, n=2)
        th = reg_a[:, 2060:2060 + 2048].rearrange("p (s t) -> p s t", s=4)
        h = reg_a[:, 2060:].rearrange("p (s n t) -> p s n t", s=HR, n=2)
        h2 = reg_a[:, 2060:].rearrange("p (s t) -> p s t", s=HR)
        d_a2 = reg_a[:, 0:2048].rearrange("p (s t) -> p s t", s=2)
        cb = reg_c
        hid = reg_c[:, 0:FT, :]
        y_sb, mem, acc, cnt = (reg_c[:, FT + 2 * j:FT + 2 * j + 2, :].rearrange("p a t -> p (a t)")
                               for j in range(4))
        xn = reg_y[:, 0:2, :].rearrange("p a (b e) -> p (a b) e", e=E)
        xnT = reg_y[:, 2:4, :]
        sp = reg_y
        yv = reg_y

        xin = sb("xin", [P, TT, E])
        xres = sb("xres", [P, TT, E])
        u2 = sb("u2", [P, DT, L])
        sz = sb("sz", [P, DT, L])
        dt = sb("dt", [P, DT, L])
        dtu = sb("dtu", [P, DT, L])
        bcs = sb("bcs", [3 * BC, L], BF16)
        bcr = sb("bcr", [3 * BC, L])
        dtin = sb("dtin", [DTR, L])
        x1 = sb("x1", [P, TT, E])
        hT = sb("hT", [P, ET, L])
        x2 = sb("x2", [P, TT, E])
        x2T = sb("x2T", [P, ET, L])
        xs = sb("xs", [P, 4, 2 * L])
        tr, tz, nh, nn = (xs[:, j, :] for j in range(4))
        sc = sb("sc", [M, L])
        an = sb("an", [M, L])
        rt = sb("rt", [M, L])
        gT = sb("gT", [P, ET, M])
        pnT = sb("pnT", [P, ET, M])
        vw = sb("vw", [M, 3 * E])
        ctxt = sb("ctxt", [M, E])
        small = sb("small", [M, 8])
        stats = {n: (sb(f"{n}_st", [P, TT, 6]), sb(f"{n}_mv", [P, TT, 2]), sb(f"{n}_var", [P, TT]),
                     sb(f"{n}_rstd", [P, TT])) for n in ("pre", "post", "x2", "out")}

        pb = ps("pb", [P, 4, L])
        py = ps("py", [P, L])
        pc = ps("pc", [P, L])
        px = ps("px", [P, 2, L])

        s = {n: ctx.enter_context(nc.semaphore(n)) for n in COUNTS}
        weights_in = ctx.enter_context(nc.semaphore("weights_in"))
        consts_done = ctx.enter_context(nc.semaphore("consts_done"))
        params_done = ctx.enter_context(nc.semaphore("params_done"))
        setup_full = ctx.enter_context(nc.semaphore("setup_full"))
        setup_copied = ctx.enter_context(nc.semaphore("setup_copied"))
        a_done = ctx.enter_context(nc.semaphore("a_done"))
        arrived = ctx.enter_context(nc.semaphore("arrived"))
        resumed = ctx.enter_context(nc.semaphore("resumed"))
        go = ctx.enter_context(nc.semaphore("go"))

        def col(name, j):
            return cols[:, COLS[name].start + j:COLS[name].start + j + 1]

        def tokens(dram, b):
            return dram[bass.ds(b, 1)].rearrange("a (i p) e -> (a p) i e", p=P)

        wq, wk, wv = (reg_c[:, j, :].rearrange("p (k n) -> p k n", k=ET) for j in range(3))
        wih = reg_c[:, 4:7, :].rearrange("p a t -> p (a t)").rearrange("p (k n) -> p k n", k=ET)

        loads = [(w_in, w_inT.rearrange("(k p) n -> p k n", p=P)), (w_x, w_xT.rearrange("(k p) n -> p k n", p=P)),
                 (w_dt, w_dtT), (w_out, w_outT.rearrange("(k p) n -> p k n", p=P)),
                 (whh, whhT.rearrange("(k p) n -> p k n", p=P)), (cols, cols_d),
                 (wq, wq_d.rearrange("(k p) n -> p k n", p=P)), (wk, wk_d.rearrange("(k p) n -> p k n", p=P)),
                 (wv, wv_d.rearrange("(k p) n -> p k n", p=P)), (wih, wihT.rearrange("(k p) n -> p k n", p=P)),
                 (w_fc, w_fcT.rearrange("(k p) n -> p k n", p=P)), (w_pr, w_prT.rearrange("(k p) n -> p k n", p=P))]

        block = ctx.enter_context(nc.Block())

        def meet(eng, nxt):
            eng.drain().then_inc(arrived, 1)
            eng.wait_ge(go, nxt)
            eng.sem_inc(resumed, 1)

        def iterations(eng, body):
            body(0, True, False, False)
            body(1, True, True, False)
            with eng.Fori(2, BATCH) as i:
                body(i, True, True, True)
            body(BATCH, False, True, True)
            body(BATCH + 1, False, False, True)

        plan = {0: [("ctx", 0)], 1: [("ctx", 1)], 2: [("ctx", 2)], 3: [("ctx", 3)]}
        for k in range(NI):
            for j in range(7):
                plan[5 + 7 * k + j] = [(("norm", "score", "soft", "renorm", "gates", "cand", "update")[j], k)]
        for j in range(4):
            plan[5 + 7 * NI + j] = [("final", j)]
        SLOTS = GROUPS + LAG

        @block.sync
        def _(sp_):
            for dst, src in loads:
                sp_.dma_start(dst[:], src).then_inc(weights_in, 16)
            sp_.dma_start(xin[:], tokens(x, 0)).then_inc(weights_in, 16)
            sp_.wait_ge(weights_in, 16 * (len(loads) + 1))
            sp_.wait_ge(arrived, 4)
            sp_.sem_clear(arrived)
            sp_.sem_inc(go, 1)

            def body(i, mamba, slots, ffn):
                waits = []
                if mamba:
                    sp_.dma_start(xres[:], tokens(x, i)).then_inc(s["xres_load"], 16)
                    sp_.wait_ge(s["pre_norm"], TT)
                    sp_.dma_start(xin[:], tokens(x, (i + 1) % BATCH)).then_inc(s["xin_load"], 16)
                    waits += ["xres_load", "xin_load"]
                if ffn:
                    sp_.wait_ge(s["out_norm"], TT)
                    sp_.dma_start(tokens(out, i - 2), acc.rearrange("p (i e) -> p i e", e=E)).then_inc(s["out_store"], 16)
                    waits += ["out_store"]
                if mamba:
                    if slots:
                        sp_.wait_ge(s["c_norm"], 1)
                        sp_.wait_ge(s["pnT_ready"], 2)
                    sp_.dma_start(ctxt[:], ctx_in[bass.ds(i, 1)].rearrange("a m e -> (a m) e")).then_inc(s["ctx_load"], 16)
                    waits += ["ctx_load"]
                for w in waits:
                    sp_.wait_ge(s[w], 16)
                sp_.wait_ge(arrived, 4)
                for n in COUNTS:
                    sp_.sem_clear(s[n])
                sp_.sem_clear(arrived)
                sp_.sem_inc(go, 1)

            iterations(sp_, body)

        @block.gpsimd
        def _(pool):
            pool.memset(ones[:], 1.0).then_inc(consts_done, 1)
            pool.memset(mhalf[:], -0.5).then_inc(consts_done, 1)
            pool.memset(rms_eps[:], RMS_EPS).then_inc(consts_done, 1)
            pool.memset(ident[:], 0.0).then_inc(consts_done, 1)
            pool.wait_ge(consts_done, 4)
            pool.affine_select(out=ident[:], in_=ident[:], compare_op=ALU.not_equal, fill=1.0, base=0,
                               pattern=[[-1, P]], channel_multiplier=1).then_inc(consts_done, 1)
            meet(pool, 1)

            def rstd(name):
                pool.wait_ge(s[f"{name}_ve"], 1)
                pool.tensor_tensor(stats[name][3][:], stats[name][2][:], mhalf[:], ALU.pow).then_inc(s[f"{name}_rs"], 1)

            def slot_step(step, k, ffn):
                if (step, k) == ("ctx", 0):
                    pool.wait_ge(s["c_ve"], 1)
                    pool.tensor_tensor(small[:, 2:3], small[:, 1:2], mhalf[0:M, 0:1], ALU.pow).then_inc(s["c_rs"], 1)
                elif step == "cand":
                    pool.wait_ge(s["n_ready"], ET * (k + 1))
                    pool.tensor_tensor(nh, hT[:].rearrange("p a t -> p (a t)"), nn, ALU.subtract).then_inc(s["d_done"], 1)
                elif (step, k) == ("final", 1):
                    rstd("x2")

            def body(i, mamba, slots, ffn):
                if mamba:
                    pool.memset(upad[:, :, 0:KC - 1], 0.0).then_inc(s["upad_zero"], 1)
                    rstd("pre")
                if ffn:
                    for f in range(FT):
                        pool.wait_ge(s["f_relu"], f + 1)
                        pool.tensor_tensor(hid[:, f], hid[:, f], hid[:, f], ALU.mult).then_inc(s["f_sq"], 1)
                if mamba:
                    pool.wait_ge(s["conv_step"], (KC - 1) * DT)
                    pool.memset(d_a[:, :, :, 0:1], 0.0).then_inc(s["da_zero"], 1)
                    for c in range(DT):
                        pool.wait_ge(s["sp_ln"], c + 1)
                        pool.tensor_tensor(dt[:, c], dt[:, c], sp[:, c], ALU.add).then_inc(s["dt_ready"], 1)
                        pool.wait_ge(s["dt_ready"], c + 1)
                        pool.tensor_tensor(dtu[:, c], dt[:, c], u2[:, c], ALU.mult).then_inc(s["dtu_ready"], 1)
                if ffn:
                    rstd("out")
                for g in range(SLOTS):
                    if mamba and g < GROUPS:
                        q = g % PAIRS
                        pool.wait_ge(s["scan_done"], g + 1)
                        pool.wait_ge(s["cb_ready"], 2 * q + 2)
                        pool.tensor_tensor(h[:, g % HR], h[:, g % HR], cb[:, 2 * q:2 * q + 2], ALU.mult).then_inc(s["hc_done"], 1)
                    if mamba and g >= LAG + PAIRS - 1 and (g - LAG) % PAIRS == PAIRS - 1:
                        c = (g - LAG) // PAIRS
                        pool.wait_ge(s["ypost_done"], c + 1)
                        pool.tensor_tensor(yv[:, c], yv[:, c], sz[:, c], ALU.mult).then_inc(s["yz_done"], 1)
                    if slots:
                        for st in plan.get(g, ()):
                            slot_step(*st, ffn)
                if mamba:
                    rstd("post")
                meet(pool, i + 2)

            iterations(pool, body)

        @block.tensor
        def _(pe):
            pe.wait_ge(weights_in, 16 * (len(loads) + 1))
            for e1 in range(ET):
                for d in range(ET):
                    mm = pe.matmul(px[:, e1, 0:E], wk[:, d, e1 * P:(e1 + 1) * P], wq[:, d, :], start=(d == 0), stop=(d == ET - 1))
            mm.then_inc(setup_full, 1)
            for e1 in range(ET):
                for j in range(2):
                    for d in range(ET):
                        mm = pe.matmul(pb[:, 2 * e1 + j, 0:384], wv[:, d, e1 * P:(e1 + 1) * P], wih[:, d, j * 384:(j + 1) * 384],
                                       start=(d == 0), stop=(d == ET - 1))
            mm.then_inc(setup_full, 1)
            meet(pe, 1)

            def slot_step(step, k, ffn):
                if step == "ctx":
                    if k == 1:
                        pe.wait_ge(s["c_norm"], 1)
                        if ffn:
                            pe.wait_ge(s["y_copied"], 1)
                        for e in range(ET):
                            mm = pe.transpose(px[:, 0, e * M:(e + 1) * M], ctxt[:, e * P:(e + 1) * P], ident[0:M, 0:M])
                        mm.then_inc(s["x_full"], 1)
                    if k == 2:
                        pe.wait_ge(s["pnT_ready"], 2)
                        for e in range(ET):
                            for d in range(ET):
                                mm = pe.matmul(px[:, 1, e * M:(e + 1) * M], mqk[:, d, e * P:(e + 1) * P], pnT[:, d],
                                               start=(d == 0), stop=(d == ET - 1))
                        mm.then_inc(s["x_full"], 1)
                    if k == 3:
                        for j in range(2):
                            if j == 1:
                                pe.wait_ge(s["g_ready"], 2)
                            for d in range(ET):
                                mm = pe.matmul(px[0:M, j, 0:384], pnT[:, d], wvih[:, d, j * 384:(j + 1) * 384],
                                               start=(d == 0), stop=(d == ET - 1))
                            mm.then_inc(s["x_full"], 1)
                    return
                f0 = 4 + 11 * k
                if step == "norm":
                    pe.wait_ge(s["vw_ready"], 2)
                    if k:
                        pe.wait_ge(s["h_done"], k)
                        pe.wait_ge(s["v2_done"], 2 * k)
                    for e in range(ET):
                        mm = pe.matmul(px[0:M, 1, :], gT[:, e], hT[:, e], start=(e == 0), stop=(e == ET - 1))
                    mm.then_inc(s["x_full"], 1)
                    pe.wait_ge(s["sq_ready"], k + 1)
                    for e in range(ET):
                        mm = pe.matmul(px[0:M, 0, :], ones[:, 0:M], nn[:, e * L:(e + 1) * L], start=(e == 0), stop=(e == ET - 1))
                    mm.then_inc(s["x_full"], 1)
                elif step == "soft":
                    pe.wait_ge(s["an0_done"], k + 1)
                    pe.wait_ge(s["lnss_done"], k + 1)
                    pe.matmul(px[0:M, 0, :], ones[0:M, :], an[:], start=True, stop=True).then_inc(s["x_full"], 1)
                elif step == "renorm":
                    pe.wait_ge(s["sc_done"], k + 1)
                    for j in range(4):
                        b = (j + 1) % 2
                        if j == 1:
                            pe.wait_ge(s["eps_done"], k + 1)
                        if j >= 2:
                            pe.wait_ge(s["trz_ready"], 4 * k + j - 1)
                        for e in range(ET):
                            pe.matmul(px[:, b, :], whh[:, e, j * P:(j + 1) * P], hT[:, e], start=(e == 0), stop=False)
                        if j == 0:
                            pe.wait_ge(s["an_done"], k + 1)
                        pe.matmul(px[:, b, :], vw[:, j * P:(j + 1) * P], an[:], start=False, stop=True).then_inc(s["x_full"], 1)
                elif step == "gates":
                    for j in range(ET):
                        b = (j + 1) % 2
                        pe.wait_ge(s["trz_ready"], 4 * k + 3 + j)
                        for e in range(ET):
                            mm = pe.matmul(px[:, b, :], whh[:, e, (4 + j) * P:(5 + j) * P], hT[:, e], start=(e == 0), stop=(e == ET - 1))
                        mm.then_inc(s["x_full"], 1)
                    for j in range(ET):
                        b = (j + 1) % 2
                        pe.wait_ge(s["nh_ready"], ET * k + j + 1)
                        pe.matmul(px[:, b, :], vw[:, (4 + j) * P:(5 + j) * P], an[:], start=True, stop=True).then_inc(s["x_full"], 1)
                elif step == "final":
                    if k == 0:
                        pe.wait_ge(s["h_done"], NI)
                        pe.wait_ge(s["v2_done"], 2 * NI)
                        for i2 in range(TT):
                            for e in range(ET):
                                o = (i2 % 2) * E + e * P
                                mm = pe.transpose(px[:, i2 // 2, o:o + P], hT[:, e, i2 * P:(i2 + 1) * P], ident[:])
                        mm.then_inc(s["x_full"], 1)
                    if k == 2:
                        pe.wait_ge(s["x2_norm"], TT)
                        for e in range(ET):
                            for i2 in range(TT):
                                mm = pe.transpose(px[:, e, i2 * P:(i2 + 1) * P], x2[:, i2, e * P:(e + 1) * P], ident[:])
                            mm.then_inc(s["x_full"], 1)

            def pre_a():
                pe.wait_ge(s["pre_norm"], TT)
                for e in range(ET):
                    for i2 in range(TT):
                        mm = pe.transpose(pb[:, e, i2 * P:(i2 + 1) * P], xn[:, i2, e * P:(e + 1) * P], ident[:])
                    mm.then_inc(s["pre_full"], 1)

            def in_proj(j):
                bank = (2 + j) % 4
                pe.wait_ge(s["xnT_ready"], 2)
                if j >= 4:
                    pe.wait_ge(s["uacc_ready"], j - 3)
                for e in range(ET):
                    mm = pe.matmul(pb[:, bank, :], w_in[:, e, j * P:(j + 1) * P], xnT[:, e], start=(e == 0), stop=(e == ET - 1))
                mm.then_inc(s["pre_full"], 1)

            def x_proj():
                pe.wait_ge(s["u_ready"], DT)
                pe.wait_ge(s["sz_ready"], 1)
                for c in range(DT):
                    mm = pe.matmul(pb[0:3 * BC, 2, :], w_x[:, c, DTR:], u2[:, c], start=(c == 0), stop=(c == DT - 1))
                mm.then_inc(s["pre_full"], 1)
                pe.wait_ge(s["sz_ready"], 2)
                for c in range(DT):
                    mm = pe.matmul(pb[0:DTR, 3, :], w_x[:, c, 0:DTR], u2[:, c], start=(c == 0), stop=(c == DT - 1))
                mm.then_inc(s["pre_full"], 1)

            def dt_proj():
                pe.wait_ge(s["dtin_ready"], 1)
                for c in range(DT):
                    pe.wait_ge(*((s["sz_ready"], 3 + c) if c < 2 else (s["bc_split"], 2)))
                    pe.matmul(pb[:, c, :], w_dt[:, c * P:(c + 1) * P], dtin[:], start=True, stop=True).then_inc(s["pre_full"], 1)

            def ffn_up(f):
                if f >= 2:
                    pe.wait_ge(s["f_relu"], f - 1)
                for e in range(ET):
                    mm = pe.matmul(px[:, f % 2, :], w_fc[:, e, f * P:(f + 1) * P], x2T[:, e], start=(e == 0), stop=(e == ET - 1))
                mm.then_inc(s["f_full"], 1)

            def ffn_down():
                pe.wait_ge(s["f_sq"], FT)
                for i2 in range(TT):
                    for f in range(FT):
                        mm = pe.matmul(px[:, i2 // 2, (i2 % 2) * E:(i2 % 2 + 1) * E], hid[:, f, i2 * P:(i2 + 1) * P], w_pr[:, f],
                                       start=(f == 0), stop=(f == FT - 1))
                mm.then_inc(s["f_full"], 1)

            def bcb(g):
                n = 2 * (g % PAIRS)
                if g < 2:
                    pe.wait_ge(s["sp_abs"], DT)
                    pe.wait_ge(s["bc_split"], 5)
                else:
                    pe.wait_ge(s["scan_done"], g - 1)
                for j in range(2):
                    mm = pe.matmul(pb[:, 2 * (g % 2) + j, :], sel[:, n + j, :], bcs[:], start=True, stop=True)
                mm.then_inc(s["bcb_full"], 1)

            def cbm(n):
                if n:
                    pe.wait_ge(s["cb_ready"], n)
                pe.matmul(pc[:], sel[:, NS + n, :], bcs[:], start=True, stop=True).then_inc(s["cb_full"], 1)

            def hsum(g):
                c, q = g // PAIRS, g % PAIRS
                pe.wait_ge(s["hc_done"], g + 1)
                if q == 0 and c:
                    pe.wait_ge(s["ypost_done"], c)
                for j in range(2):
                    mm = pe.matmul(py[:], ident[:], h[:, g % HR, j], start=(q == 0 and j == 0), stop=(q == PAIRS - 1 and j == 1))
                mm.then_inc(s["hsum_done"], 1)

            def body(i, mamba, slots, ffn):
                if mamba:
                    pre_a()
                if ffn:
                    ffn_up(0)
                    ffn_up(1)
                for j in range(2 * DT):
                    if mamba:
                        in_proj(j)
                    if ffn and j < FT - 2:
                        ffn_up(j + 2)
                if mamba:
                    x_proj()
                    dt_proj()
                if ffn:
                    ffn_down()
                for g in range(SLOTS):
                    if mamba:
                        if g == 0:
                            bcb(0)
                            cbm(0)
                            cbm(1)
                        if g + 1 < GROUPS:
                            bcb(g + 1)
                        if g + 1 < PAIRS:
                            cbm(2 * g + 2)
                            cbm(2 * g + 3)
                        if g >= LAG:
                            hsum(g - LAG)
                    if slots:
                        for st in plan.get(g, ()):
                            slot_step(*st, ffn)
                if mamba:
                    pe.wait_ge(s["scan_done"], GROUPS)
                    pe.wait_ge(s["yz_done"], DT)
                    for i2 in range(TT):
                        for c in range(DT):
                            mm = pe.matmul(pb[:, i2, 0:E], yv[:, c, i2 * P:(i2 + 1) * P], w_out[:, c], start=(c == 0), stop=(c == DT - 1))
                        mm.then_inc(s["op_full"], 1)
                    pe.wait_ge(s["post_norm"], TT)
                    for e in range(ET):
                        for i2 in range(TT):
                            mm = pe.transpose(pb[:, e, i2 * P:(i2 + 1) * P], x1[:, i2, e * P:(e + 1) * P], ident[:])
                        mm.then_inc(s["post_full"], 1)
                meet(pe, i + 2)

            iterations(pe, body)

        @block.scalar
        def _(act):
            act.wait_ge(weights_in, 16 * (len(loads) + 1))
            act.activation(neg_a[:], cols[:, COLS["A_log"]], ACT.Exp).then_inc(a_done, 1)
            act.wait_ge(setup_full, 1)
            act.activation(mqk[:], px[:, :, 0:E], ACT.Copy).then_inc(setup_copied, 1)
            act.wait_ge(setup_full, 2)
            act.activation(wvih[:].rearrange("p e (j n) -> p (e j) n", n=384), pb[:, :, 0:384], ACT.Copy).then_inc(setup_copied, 1)
            meet(act, 1)

            def slot_step(step, k, ffn):
                if step == "ctx":
                    if k == 0:
                        act.activation(nh[0:M, 0:E], ctxt[:], ACT.Square, accum_out=small[:, 0:1]).then_inc(s["c_sq"], 1)
                    if k == 1:
                        act.wait_ge(s["x_full"], 1)
                        for e in range(ET):
                            act.activation(pnT[:, e], px[:, 0, e * M:(e + 1) * M], ACT.Copy, scale=col("input_w", e)).then_inc(s["pnT_ready"], 1)
                    if k == 2:
                        act.wait_ge(s["x_full"], 2)
                        for e in range(ET):
                            act.activation(gT[:, e], px[:, 1, e * M:(e + 1) * M], ACT.Copy, scale=g_scale[:, e:e + 1]).then_inc(s["g_ready"], 1)
                    if k == 3:
                        for j in range(2):
                            act.wait_ge(s["x_full"], 3 + j)
                            act.activation(vw[:, j * 384:(j + 1) * 384], px[0:M, j, 0:384], ACT.Copy).then_inc(s["vw_ready"], 1)
                    return
                f0 = 4 + 11 * k
                if step == "norm":
                    if k:
                        act.wait_ge(s["h_done"], k)
                    act.activation(nn, hT[:].rearrange("p a t -> p (a t)"), ACT.Square).then_inc(s["sq_ready"], 1)
                    act.wait_ge(s["x_full"], f0 + 2)
                    act.activation(rt[:], px[0:M, 0, :], ACT.Ln, scale=1.0 / E, bias=rms_eps[0:M, :]).then_inc(s["lnss_done"], 1)
                    act.wait_ge(s["lnss_done"], k + 1)
                    act.activation(rt[:], rt[:], ACT.Exp, scale=-0.5).then_inc(s["rsb_done"], 1)
                elif step == "score":
                    act.wait_ge(s["nmx_done"], k + 1)
                    act.activation(sc[:], sc[:], ACT.Exp, bias=small[:, 4:5], accum_out=small[:, 5:6]).then_inc(s["ex_done"], 1)
                elif step == "renorm":
                    for j in range(4):
                        act.wait_ge(s["x_full"], f0 + 4 + j)
                        act.activation(xs[:, j // 2, (j % 2) * L:(j % 2 + 1) * L], px[:, (j + 1) % 2, :], ACT.Tanh, scale=0.5,
                                       bias=half_b[:, j:j + 1]).then_inc(s["trz_ready"], 1)
                elif step == "gates":
                    for j in range(ET):
                        act.wait_ge(s["x_full"], f0 + 8 + j)
                        act.activation(nh[:, j * L:(j + 1) * L], px[:, (j + 1) % 2, :], ACT.Identity, scale=0.5,
                                       bias=half_b[:, 4 + j:5 + j]).then_inc(s["nh_ready"], 1)
                elif step == "cand":
                    for j in range(ET):
                        act.wait_ge(s["v2_done"], ET * k + j + 1)
                        act.activation(nn[:, j * L:(j + 1) * L], nh[:, j * L:(j + 1) * L], ACT.Tanh,
                                       bias=col("bih", 4 + j)).then_inc(s["n_ready"], 1)
                elif step == "final" and k == 3:
                    for e in range(ET):
                        act.wait_ge(s["x_full"], 4 + 11 * NI + 2 + e)
                        act.activation(x2T[:, e], px[:, e, :], ACT.Copy).then_inc(s["x2T_ready"], 1)

            def body(i, mamba, slots, ffn):
                def relu(f):
                    act.wait_ge(s["f_full"], f + 1)
                    act.activation(hid[:, f], px[:, f % 2, :], ACT.Relu).then_inc(s["f_relu"], 1)

                if mamba:
                    for e in range(ET):
                        act.wait_ge(s["pre_full"], e + 1)
                        act.activation(xnT[:, e], pb[:, e, :], ACT.Identity, scale=col("ln_g", e), bias=col("ln_b", e)).then_inc(s["xnT_ready"], 1)
                if ffn:
                    relu(0)
                    relu(1)
                if mamba:
                    act.wait_ge(s["upad_zero"], 1)
                for j in range(DT):
                    if mamba:
                        act.wait_ge(s["pre_full"], 3 + j)
                        act.activation(upad[:, j, KC - 1:], pb[:, (2 + j) % 4, :], ACT.Copy)
                        act.activation(u2[:, j], pb[:, (2 + j) % 4, :], ACT.Identity, scale=col("conv_w", j * KC + KC - 1),
                                       bias=col("conv_b", j)).then_inc(s["uacc_ready"], 1)
                    if ffn:
                        relu(j + 2)
                for j in range(DT):
                    if mamba:
                        act.wait_ge(s["conv_step"], 6 * (j // 2) + 5 + j % 2)
                        if j >= 2:
                            act.wait_ge(s["u_ready"], j - 1)
                        act.activation(th[:, j % 2], u2[:, j], ACT.Tanh, scale=0.5).then_inc(s["uth_ready"], 1)
                        act.wait_ge(s["pre_full"], 7 + j)
                        if j >= 2:
                            act.wait_ge(s["sz_ready"], j - 1)
                        act.activation(th[:, 2 + j % 2], pb[:, (2 + j) % 4, :], ACT.Tanh, scale=0.5).then_inc(s["zth_ready"], 1)
                    if ffn and j < 2:
                        relu(j + 6)
                if mamba:
                    act.wait_ge(s["pre_full"], 12)
                    act.activation(dtin[:], pb[0:DTR, 3, :], ACT.Copy).then_inc(s["dtin_ready"], 1)
                    for c in range(DT):
                        act.wait_ge(s["pre_full"], 13 + c)
                        act.activation(dt[:, c], pb[:, c, :], ACT.Relu, bias=col("dt_bias", c))
                        act.activation(sp[:, c], pb[:, c, :], ACT.Abs, bias=col("dt_bias", c)).then_inc(s["sp_abs"], 1)
                    act.wait_ge(s["sp_abs"], DT)
                    act.activation(sp[:], sp[:], ACT.Exp, scale=-1.0).then_inc(s["sp_exp"], 1)
                    act.wait_ge(s["sp_exp"], 1)
                    for c in range(DT):
                        act.activation(sp[:, c], sp[:, c], ACT.Ln, bias=1.0).then_inc(s["sp_ln"], 1)

                def cb_copy(n):
                    if ffn and n == 0:
                        act.wait_ge(s["f_full"], FT + 1)
                    if ffn and n == NS // 2:
                        act.wait_ge(s["out_store"], 16)
                    act.wait_ge(s["cb_full"], n + 1)
                    act.activation(cb[:, n], pc[:], ACT.Copy).then_inc(s["cb_ready"], 1)

                def decay(g):
                    c, n = g // PAIRS, 2 * (g % PAIRS)
                    if g == 0:
                        act.wait_ge(s["da_zero"], 1)
                    if g % PAIRS == 0:
                        act.wait_ge(s["dt_ready"], c + 1)
                    if g >= 2:
                        act.wait_ge(s["scan_done"], g - 1)
                    for j in range(2):
                        ins = act.activation(d_a[:, g % 2, j, 1:], dt[:, c, 1:], ACT.Exp, scale=neg_a[:, c * NS + n + j:c * NS + n + j + 1])
                    ins.then_inc(s["da_ready"], 1)

                for g in range(SLOTS):
                    if mamba:
                        if g == 0:
                            decay(0)
                            cb_copy(0)
                            cb_copy(1)
                        if g + 1 < GROUPS:
                            decay(g + 1)
                        if g + 1 < PAIRS:
                            cb_copy(2 * g + 2)
                            cb_copy(2 * g + 3)
                    if slots:
                        for st in plan.get(g, ()):
                            slot_step(*st, ffn)
                if mamba:
                    if slots:
                        act.wait_ge(s["x_full"], 4 + 11 * NI + 1)
                    for e in range(ET):
                        act.wait_ge(s["post_full"], e + 1)
                        act.activation(hT[:, e], pb[:, e, :], ACT.Copy).then_inc(s["hT_loaded"], 1)
                meet(act, i + 2)

            iterations(act, body)

        @block.vector
        def _(dve):
            dve.wait_ge(weights_in, 16 * (len(loads) + 1))
            dve.wait_ge(a_done, 1)
            dve.wait_ge(consts_done, 5)
            dve.tensor_scalar(neg_a[:], neg_a[:], -1.0, None, ALU.mult)
            dve.tensor_tensor(half_b[:], cols[:, COLS["bih"]], cols[:, COLS["bhh"]], ALU.add).then_inc(params_done, 1)
            dve.wait_ge(params_done, 1)
            dve.tensor_copy(half_b[:, 4:6], cols[:, COLS["bhh"].start + 4:COLS["bhh"].start + 6]).then_inc(params_done, 1)
            dve.wait_ge(params_done, 2)
            dve.tensor_scalar(half_b[:], half_b[:], 0.5, None, ALU.mult)
            dve.tensor_scalar(half_d[:], cols[:, COLS["D"]], 0.5, None, ALU.mult)
            dve.tensor_scalar(g_scale[:], cols[:, COLS["slot_w"]], SCALE, None, ALU.mult)
            dve.tensor_scalar(w_out[:], w_out[:], 0.5, None, ALU.mult)
            dve.tensor_scalar(w_x[:, :, 0:DTR], w_x[:, :, 0:DTR], 0.5, None, ALU.mult)
            for r in range(3):
                o = DTR + r * BC
                dve.tensor_scalar(w_x[:, :, o:o + NS], w_x[:, :, o:o + NS], 0.25, None, ALU.mult)
                dve.tensor_scalar(w_x[:, :, o + NS:o + BC], w_x[:, :, o + NS:o + BC], 0.5, None, ALU.mult)
            dve.tensor_tensor(sel32[:], ident[0:3 * BC, 0:BC], ident[0:3 * BC, BC:2 * BC], ALU.add).then_inc(params_done, 1)
            dve.wait_ge(params_done, 3)
            dve.tensor_tensor(sel32[:], sel32[:], ident[0:3 * BC, 2 * BC:3 * BC], ALU.add).then_inc(params_done, 1)
            dve.wait_ge(params_done, 4)
            dve.tensor_copy(sel[:], sel32[:].unsqueeze(2).to_broadcast([3 * BC, BC, P]))
            meet(dve, 1)

            def norm_stats(name, src):
                st, mv, var, _ = stats[name]
                for i2 in range(TT):
                    dve.bn_stats(st[:, i2], src[:, i2]).then_inc(s[f"{name}_stat"], 1)
                dve.wait_ge(s[f"{name}_stat"], TT)
                for i2 in range(TT):
                    dve.bn_aggr(mv[:, i2], st[:, i2]).then_inc(s[f"{name}_aggr"], 1)
                dve.wait_ge(s[f"{name}_aggr"], TT)
                dve.tensor_scalar(var[:], mv[:, :, 1], LN_EPS, None, ALU.add).then_inc(s[f"{name}_ve"], 1)

            def norm_apply(name, src, dst):
                _, mv, _, rstd = stats[name]
                dve.wait_ge(s[f"{name}_rs"], 1)
                for i2 in range(TT):
                    dve.tensor_scalar(dst[:, i2], src[:, i2], mv[:, i2, 0:1], rstd[:, i2:i2 + 1], ALU.subtract,
                                      ALU.mult).then_inc(s[f"{name}_norm"], 1)

            def slot_step(step, k, ffn):
                if step == "ctx":
                    if k == 0:
                        dve.wait_ge(s["c_sq"], 1)
                        dve.tensor_scalar(small[:, 1:2], small[:, 0:1], 1.0 / E, RMS_EPS, ALU.mult, ALU.add).then_inc(s["c_ve"], 1)
                    if k == 1:
                        dve.wait_ge(s["c_rs"], 1)
                        dve.tensor_scalar(ctxt[:], ctxt[:], small[:, 2:3], None, ALU.mult).then_inc(s["c_norm"], 1)
                    return
                f0 = 4 + 11 * k
                if step == "score":
                    dve.wait_ge(s["rsb_done"], k + 1)
                    dve.tensor_tensor(sc[:], px[0:M, 1, :], rt[:], ALU.mult).then_inc(s["sc_done"], 1)
                    dve.wait_ge(s["sc_done"], k + 1)
                    dve.tensor_reduce(small[:, 3:4], sc[:], AX.X, ALU.max).then_inc(s["mx_done"], 1)
                    dve.wait_ge(s["mx_done"], k + 1)
                    dve.tensor_scalar(small[:, 4:5], small[:, 3:4], -1.0, None, ALU.mult).then_inc(s["nmx_done"], 1)
                elif step == "soft":
                    dve.wait_ge(s["ex_done"], k + 1)
                    dve.reciprocal(small[:, 6:7], small[:, 5:6]).then_inc(s["rz_done"], 1)
                    dve.wait_ge(s["rz_done"], k + 1)
                    dve.tensor_scalar(an[:], sc[:], small[:, 6:7], None, ALU.mult).then_inc(s["an0_done"], 1)
                elif step == "renorm":
                    dve.wait_ge(s["x_full"], f0 + 3)
                    dve.tensor_scalar(rt[:], px[0:M, 0, :], RMS_EPS, None, ALU.add).then_inc(s["eps_done"], 1)
                    dve.wait_ge(s["eps_done"], k + 1)
                    dve.reciprocal(rt[:], rt[:]).then_inc(s["rt_done"], 1)
                    dve.wait_ge(s["rt_done"], k + 1)
                    dve.tensor_tensor(an[:], an[:], rt[:], ALU.mult).then_inc(s["an_done"], 1)
                elif step == "cand":
                    dve.wait_ge(s["nh_ready"], ET * (k + 1))
                    dve.scalar_tensor_tensor(nh, tr, 1.0, nh, ALU.add, ALU.mult).then_inc(s["v1_done"], 1)
                    dve.wait_ge(s["v1_done"], k + 1)
                    for j in range(ET):
                        dve.wait_ge(s["x_full"], f0 + 10 + j)
                        dve.tensor_tensor(nh[:, j * L:(j + 1) * L], nh[:, j * L:(j + 1) * L], px[:, (j + 1) % 2, :],
                                          ALU.add).then_inc(s["v2_done"], 1)
                elif step == "update":
                    dve.wait_ge(s["d_done"], k + 1)
                    dve.scalar_tensor_tensor(nh, tz, 1.0, nh, ALU.add, ALU.mult).then_inc(s["e_done"], 1)
                    dve.wait_ge(s["e_done"], k + 1)
                    dve.scalar_tensor_tensor(hT[:].rearrange("p a t -> p (a t)"), nh, 0.5, nn, ALU.mult, ALU.add).then_inc(s["h_done"], 1)
                elif step == "final":
                    x2v = x2[:].rearrange("p i e -> p (i e)")
                    if k == 0:
                        dve.wait_ge(s["x_full"], 4 + 11 * NI + 1)
                        dve.tensor_tensor(x2v, px[:].rearrange("p a t -> p (a t)"), x1[:].rearrange("p i e -> p (i e)"),
                                          ALU.add).then_inc(s["xs_done"], 1)
                        dve.wait_ge(s["xs_done"], 1)
                        norm_stats("x2", x2)
                    if k == 1:
                        norm_apply("x2", x2, x2)

            def spikes():
                n = [0]

                def step(ins):
                    ins.then_inc(s["spike"], 1)
                    n[0] += 1
                    dve.wait_ge(s["spike"], n[0])

                dve.wait_ge(s["f_full"], FT + 1)
                dve.tensor_copy(y_sb, px[:].rearrange("p a t -> p (a t)")).then_inc(s["y_copied"], 1)
                dve.wait_ge(s["y_copied"], 1)
                step(dve.tensor_scalar(cnt, y_sb, THRESHOLD, None, ALU.is_gt))
                for t in range(STEPS - 1):
                    old = mem if t else y_sb
                    step(dve.scalar_tensor_tensor(acc, old, BETA, y_sb, ALU.mult, ALU.add))
                    step(dve.scalar_tensor_tensor(mem, old, THRESHOLD, acc, ALU.is_gt, ALU.subtract, reverse1=True))
                    step(dve.scalar_tensor_tensor(cnt, mem, THRESHOLD, cnt, ALU.is_gt, ALU.add))
                dve.scalar_tensor_tensor(mem, cnt, 1.0 / STEPS, x2[:].rearrange("p i e -> p (i e)"), ALU.mult,
                                         ALU.add).then_inc(s["out_res"], 1)
                dve.wait_ge(s["out_res"], 1)

            memv = mem.rearrange("p (i e) -> p i e", e=E)
            accv = acc.rearrange("p (i e) -> p i e", e=E)

            def body(i, mamba, slots, ffn):
                if mamba:
                    norm_stats("pre", xin)
                    norm_apply("pre", xin, xn)
                    for c0 in (0, 2):
                        for t in range(KC - 1):
                            for c in (c0, c0 + 1):
                                if t == 0:
                                    dve.wait_ge(s["uacc_ready"], c + 1)
                                else:
                                    dve.wait_ge(s["conv_step"], 3 * c0 + 2 * t + c - c0 - 1)
                                dve.scalar_tensor_tensor(u2[:, c], upad[:, c, t:t + L], col("conv_w", c * KC + t), u2[:, c],
                                                         ALU.mult, ALU.add).then_inc(s["conv_step"], 1)
                    for c in range(DT):
                        dve.wait_ge(s["uth_ready"], c + 1)
                        dve.scalar_tensor_tensor(u2[:, c], th[:, c % 2], 1.0, u2[:, c], ALU.add, ALU.mult).then_inc(s["u_ready"], 1)
                        dve.wait_ge(s["zth_ready"], c + 1)
                        dve.scalar_tensor_tensor(sz[:, c], th[:, 2 + c % 2], 1.0, pb[:, (2 + c) % 4, :], ALU.add, ALU.mult).then_inc(s["sz_ready"], 1)
                    dve.wait_ge(s["pre_full"], 11)
                    dve.tensor_copy(bcs[:], pb[0:3 * BC, 2, :]).then_inc(s["bc_split"], 1)
                    dve.wait_ge(s["bc_split"], 1)
                    dve.tensor_tensor(bcr[:], pb[0:3 * BC, 2, :], bcs[:], ALU.subtract).then_inc(s["bc_split"], 1)
                    dve.wait_ge(s["bc_split"], 2)
                    dve.tensor_copy(bcs[BC:2 * BC], bcr[BC:2 * BC]).then_inc(s["bc_split"], 1)
                    dve.tensor_copy(bcs[2 * BC:3 * BC], bcr[2 * BC:3 * BC]).then_inc(s["bc_split"], 1)
                    dve.wait_ge(s["bc_split"], 4)
                    dve.tensor_tensor(bcs[2 * BC:3 * BC], bcr[2 * BC:3 * BC], bcs[2 * BC:3 * BC], ALU.subtract).then_inc(s["bc_split"], 1)
                if ffn:
                    spikes()
                    norm_stats("out", memv)
                    norm_apply("out", memv, accv)

                def mul(g):
                    c, b = g // PAIRS, 2 * (g % 2)
                    dve.wait_ge(s["bcb_full"], g + 1)
                    if g % PAIRS == 0:
                        dve.wait_ge(s["dtu_ready"], c + 1)
                    dve.tensor_tensor(pb[:, b:b + 2, :], pb[:, b:b + 2, :], dtu[:, c:c + 1, :].to_broadcast([P, 2, L]),
                                      ALU.mult).then_inc(s["mul_done"], 1)

                def scan(g):
                    b = 2 * (g % 2)
                    dve.wait_ge(s["da_ready"], g + 1)
                    dve.wait_ge(s["mul_done"], g + 1)
                    if g >= HR:
                        dve.wait_ge(s["hsum_done"], g - HR + 1)
                    dve.tensor_tensor_scan(h2[:, g % HR], d_a2[:, g % 2], pb[:, b:b + 2, :].rearrange("p a t -> p (a t)"), 0.0,
                                           ALU.mult, ALU.add).then_inc(s["scan_done"], 1)

                for g in range(SLOTS):
                    if mamba:
                        if g == 0:
                            mul(0)
                        if g + 1 < GROUPS:
                            mul(g + 1)
                        if g < GROUPS:
                            scan(g)
                        if g >= LAG + PAIRS - 1 and (g - LAG) % PAIRS == PAIRS - 1:
                            c = (g - LAG) // PAIRS
                            dve.wait_ge(s["hsum_done"], PAIRS * (c + 1))
                            dve.wait_ge(s["dt_ready"], DT)
                            dve.scalar_tensor_tensor(yv[:, c], u2[:, c], half_d[:, c:c + 1], py[:], ALU.mult, ALU.add).then_inc(s["ypost_done"], 1)
                    if slots:
                        for st in plan.get(g, ()):
                            slot_step(*st, ffn)
                if mamba:
                    dve.wait_ge(s["xres_load"], 16)
                    for i2 in range(TT):
                        dve.wait_ge(s["op_full"], i2 + 1)
                        dve.scalar_tensor_tensor(xres[:, i2], xres[:, i2], 2.0, pb[:, i2, 0:E], ALU.mult, ALU.add).then_inc(s["res_done"], 1)
                    dve.wait_ge(s["res_done"], TT)
                    norm_stats("post", xres)
                    norm_apply("post", xres, x1)
                meet(dve, i + 2)

            iterations(dve, body)


def kernel(**inputs):
    import numpy as np
    import concourse.bacc as bacc
    from concourse.bass_utils import run_bass_kernel_spmd

    def rows(a, n):
        a = np.asarray(a).reshape(n, P, -1)
        return a.transpose(1, 0, 2).reshape(P, -1)

    w = {k: np.asarray(v) for k, v in inputs.items()}
    w_x = w["L0_attn_W_x"].T
    cols = np.concatenate([rows(w["L0_attn_conv_w"], DT), rows(w["L0_attn_conv_b"], DT), rows(w["L0_attn_dt_bias"], DT),
                           rows(w["L0_attn_A_log"], DT), rows(w["L0_attn_D"], DT), rows(w["L0_xattn_gru_bih"], 6),
                           rows(w["L0_xattn_gru_bhh"], 6), rows(w["L0_xattn_slot_norm_w"], ET),
                           rows(w["L0_xattn_input_norm_w"], ET), rows(w["L0_attn_ln_g"], ET), rows(w["L0_attn_ln_b"], ET)], axis=1)
    arrays = {
        "x_in": w["x"], "ctx_in": w["ctx_1024"], "cols_in": cols,
        "w_inT_in": w["L0_attn_W_in"].T,
        "w_xT_in": np.concatenate([w_x[:, :DTR]] + [w_x[:, DTR:]] * 3, axis=1),
        "w_dtT_in": w["L0_attn_W_dt"].T, "w_outT_in": w["L0_attn_W_out"].T,
        "wq_in": w["L0_xattn_Wq"], "wk_in": w["L0_xattn_Wk"], "wv_in": w["L0_xattn_Wv"],
        "wihT_in": w["L0_xattn_gru_wih"].T, "whhT_in": w["L0_xattn_gru_whh"].T,
        "w_fcT_in": w["L0_ffn_W_fc"].T, "w_prT_in": w["L0_ffn_W_proj"].T,
    }
    arrays = {k: np.ascontiguousarray(v) for k, v in arrays.items()}
    nc = bacc.Bacc("TRN2", target_bir_lowering=False, num_devices=1)
    args = [nc.dram_tensor(k, a.shape, F32, kind="ExternalInput").ap() for k, a in arrays.items()]
    out = nc.dram_tensor("x_out", (BATCH, L, E), F32, kind="ExternalOutput").ap()
    decoder_layer(nc, *args, out)
    r = run_bass_kernel_spmd(nc, [arrays], core_ids=[0])
    return r.results[0]["x_out"]
```

```python
from contextlib import ExitStack

import concourse.bass as bass
from concourse import mybir

F32 = mybir.dt.float32
BF16 = mybir.dt.bfloat16
ALU = mybir.AluOpType
ACT = mybir.ActivationFunctionType
AX = mybir.AxisListType

P = 128
BATCH, L, E = 8, 512, 256
DIN, NS, DTR, KC = 512, 16, 16, 4
M = 64
F = 4 * E
NI = 3
ET, DT, FT, TT = E // P, DIN // P, F // P, L // P
BC = 2 * NS
PAIRS = NS // 2
GROUPS = DT * PAIRS
LAG = 2
SCALE = float(E) ** -0.5
LN_EPS, RMS_EPS = 1e-5, 1e-6
BETA, THRESHOLD, STEPS = 0.9, 1.0, 5
HR = 3

COLS = {}
_at = 0
for _name, _n in (("conv_w", DT * KC), ("conv_b", DT), ("dt_bias", DT), ("A_log", DT * NS), ("D", DT),
                  ("bih", 6), ("bhh", 6), ("slot_w", ET), ("input_w", ET), ("ln_g", ET), ("ln_b", ET)):
    COLS[_name] = slice(_at, _at + _n)
    _at += _n
NCOLS = _at

COUNTS = """
pre_stat pre_aggr pre_ve pre_rs pre_norm pre_full xnT_ready upad_zero uacc_ready conv_step uth_ready u_ready
z_full zth_ready sz_ready bc_split dtin_ready sp_abs sp_exp sp_ln dt_ready dtu_ready da_zero yt_ready yback_full
cb_full cb_ready bcb_full da_ready mul_done scan_done hc_done hsum_done ypost_done yz_done
op_full res_done post_stat post_aggr post_ve post_rs post_norm post_full hT_loaded
c_sq c_ve c_rs c_norm x_full pnT_ready g_ready vw_ready sq_ready lnss_done rsb_done sc_done mx_done nmx_done ex_done
rz_done an0_done lnv_done rt_done eps_done newton_done an_done trz_ready nh_ready v1_done v2_done n_ready d_done e_done h_done
xs_done x2_stat x2_aggr x2_ve x2_rs x2_norm x2T_ready
f_full f_relu f_sq fd_full y_copied spike out_res out_stat out_aggr out_ve out_rs out_norm
xin_load xres_load ctx_load out_store
""".split()


def decoder_layer(nc, x, ctx_in, cols_d, w_inT, w_xT, w_dtT, w_outT, wq_d, wk_d, wv_d, wihT, whhT, w_fcT, w_prT, out):
    with ExitStack() as ctx:
        def sb(name, shape, dt=F32):
            return ctx.enter_context(nc.sbuf_tensor(name, shape, dt))

        def ps(name, shape):
            return ctx.enter_context(nc.psum_tensor(name, shape, F32))

        w_in = sb("w_in", [P, ET, 2 * DIN])
        w_x = sb("w_x", [P, DT, DTR + 3 * BC])
        w_dt = sb("w_dt", [3 * BC + DTR, DIN])[3 * BC:, :]
        w_out = sb("w_out", [P, DT, E])
        whh = sb("whh", [P, ET, 3 * E])
        wvih = sb("wvih", [P, ET, 3 * E])
        mqk = sb("mqk", [P, ET, E])
        w_fc = sb("w_fc", [P, ET, F])
        w_pr = sb("w_pr", [P, FT, E])
        cols = sb("cols", [P, NCOLS])
        neg_a = sb("neg_a", [P, DT * NS])
        half_b = sb("half_b", [P, 6])
        half_d = sb("half_d", [P, DT])
        g_scale = sb("g_scale", [P, ET])
        ident = sb("ident", [P, P])
        ones = sb("ones", [P, M])
        mhalf = sb("mhalf", [P, TT])
        rms_eps = sb("rms_eps", [P, 1])
        sel32 = sb("sel32", [3 * BC, BC])
        sel = sb("sel", [3 * BC, BC], BF16)

        reg_a = sb("reg_a", [P, 2060 + HR * 1024])
        reg_y = sb("reg_y", [P, DT, L])
        upad = reg_a[:, 0:2060].rearrange("p (c t) -> p c t", c=DT)
        d_a = reg_a[:, 0:2048].rearrange("p (s n t) -> p s n t", s=2, n=2)
        th = reg_a[:, 2060:2060 + 2048].rearrange("p (s t) -> p s t", s=4)
        h = reg_a[:, 2060:].rearrange("p (s n t) -> p s n t", s=HR, n=2)
        h2 = reg_a[:, 2060:].rearrange("p (s t) -> p s t", s=HR)
        d_a2 = reg_a[:, 0:2048].rearrange("p (s t) -> p s t", s=2)
        bcr = reg_a[0:3 * BC, 0:L]
        dtin = reg_a[3 * BC:3 * BC + DTR, L:2 * L]
        xn = reg_y[:, 0:2, :].rearrange("p a (b e) -> p (a b) e", e=E)
        xnT = reg_y[:, 2:4, :]
        sp = reg_y
        yv = reg_y

        xin = sb("xin", [P, TT, E])
        xres = sb("xres", [P, TT, E])
        u2 = sb("u2", [P, DT, L])
        sz = sb("sz", [P, DT, L])
        dt = sb("dt", [P, DT, L])
        dtu = sb("dtu", [P, DT, L])
        cb = sb("cb", [P, NS, L])
        bcs = sb("bcs", [3 * BC, L], BF16)
        x1 = sb("x1", [P, TT, E])
        hT = sb("hT", [P, ET, L])
        x2 = sb("x2", [P, TT, E])
        x2T = sb("x2T", [P, ET, L])
        xs = sb("xs", [P, 4, 2 * L])
        tr, tz, nh, nn = (xs[:, j, :] for j in range(4))
        hid = xs[:].rearrange("p a (b t) -> p (a b) t", b=2)
        y_sb, mem, acc = (sb(n, [P, 2 * L])[:] for n in ("y_sb", "mem", "acc"))
        cnt = sb("cnt", [P, 2 * L], BF16)[:]
        sc = sb("sc", [M, L])
        an = sb("an", [M, L])
        rt = sb("rt", [M, L])
        gT = sb("gT", [P, ET, M])
        pnT = sb("pnT", [P, ET, M])
        vw = sb("vw", [M, 3 * E])
        ctxt = sb("ctxt", [M, E])
        small = sb("small", [M, 8])
        stats = {n: (sb(f"{n}_st", [P, TT, 6]), sb(f"{n}_mv", [P, TT, 2]), sb(f"{n}_var", [P, TT]),
                     sb(f"{n}_rstd", [P, TT])) for n in ("pre", "post", "x2", "out")}

        pb = ps("pb", [P, 4, L])
        py = ps("py", [P, L])
        pc = ps("pc", [P, L])
        px = ps("px", [P, 2, L])

        s = {n: ctx.enter_context(nc.semaphore(n)) for n in COUNTS}
        late_weights_in = ctx.enter_context(nc.semaphore("late_weights_in"))
        weights_in = ctx.enter_context(nc.semaphore("weights_in"))
        consts_done = ctx.enter_context(nc.semaphore("consts_done"))
        params_done = ctx.enter_context(nc.semaphore("params_done"))
        setup_full = ctx.enter_context(nc.semaphore("setup_full"))
        setup_copied = ctx.enter_context(nc.semaphore("setup_copied"))
        a_done = ctx.enter_context(nc.semaphore("a_done"))
        arrived = ctx.enter_context(nc.semaphore("arrived"))
        resumed = ctx.enter_context(nc.semaphore("resumed"))
        go = ctx.enter_context(nc.semaphore("go"))

        def col(name, j):
            return cols[:, COLS[name].start + j:COLS[name].start + j + 1]

        def tokens(dram, b):
            return dram[bass.ds(b, 1)].rearrange("a (i p) e -> (a p) i e", p=P)

        wq, wk, wv = (xs[:, 0:2, :].rearrange("p a (b t) -> p (a b) t", b=2)[:, j, :].rearrange("p (k n) -> p k n", k=ET) for j in range(3))
        wih = xs[:, 2:4, :].rearrange("p a t -> p (a t)")[:, 0:ET * 3 * E].rearrange("p (k n) -> p k n", k=ET)

        def k_rows(w):
            return w.rearrange("(k p) n -> p k n", p=P)

        loads = [(xin, tokens(x, 0)), (cols, cols_d), (w_in, k_rows(w_inT)), (w_x, k_rows(w_xT)), (w_dt, w_dtT)]
        late_loads = [(w_out, k_rows(w_outT)), (wq, k_rows(wq_d)), (wk, k_rows(wk_d)), (wv, k_rows(wv_d)),
                      (wih, k_rows(wihT)), (whh, k_rows(whhT)), (w_fc, k_rows(w_fcT)), (w_pr, k_rows(w_prT))]
        MERGE_SLOT = 10

        block = ctx.enter_context(nc.Block())

        def meet(eng, nxt):
            eng.drain().then_inc(arrived, 1)
            eng.wait_ge(go, nxt)
            eng.sem_inc(resumed, 1)

        def iterations(eng, body):
            body(0, True, False, False)
            body(1, True, True, False)
            with eng.Fori(2, BATCH) as i:
                body(i, True, True, True)
            body(BATCH, False, True, True)
            body(BATCH + 1, False, False, True)

        SLOTS = GROUPS + LAG + 1
        SPIKE_OPS = 2 + 3 * (STEPS - 1)
        plan = {}

        def place(position, *steps):
            plan.setdefault(position, []).extend(steps)

        def place_round(k, positions):
            parts = ([("norm", k)], [("score", k)], [("soft", k)], [("renorm", k), ("gate", k, 0)], [("gate", k, 1)],
                     [("gate", k, 2)], [("gate", k, 3)], [("cand_h", k, 0)], [("cand_h", k, 1), ("cand_x", k, 0)],
                     [("cand_x", k, 1), ("cand", k)], [("update", k)])
            for position, part in zip(positions, parts):
                place(position, *part)

        place("start", ("ctx", 0))
        place("norm", ("ctx", 1), *(("spike", n) for n in range(3)))
        place("u", ("ctx", 2), ("ctx", 3))
        place_round(0, ("z", "x", "x", "dt", "dt", "dt", 0, 1, 2, 3, 4))
        place("x", *(("spike", n) for n in range(3, 8)))
        place("dt", *(("spike", n) for n in range(8, SPIKE_OPS)))
        place(0, ("out_stats",))
        place(2, ("out_norm",))
        place_round(1, range(5, 16))
        place_round(2, range(16, 27))
        place(27, ("final", 0), ("final", 1))
        place(28, ("final", 2), ("final", 3))
        place(24, ("next_stats",))
        for f in range(FT):
            place(min(29 + f, SLOTS - 1), ("up", f))
        FFN_STEPS, MAMBA_STEPS = ("spike", "out_stats", "out_norm"), ("next_stats",)

        def take(position, slot_step, mamba, slots, ffn):
            for step in plan.get(position, ()):
                if ffn if step[0] in FFN_STEPS else mamba if step[0] in MAMBA_STEPS else slots:
                    slot_step(*step)

        def chunk_end(g):
            c, r = divmod(g - LAG, PAIRS)
            return c - 1 if 1 <= c <= DT and r == 0 else None

        @block.sync
        def _(sp_):
            for dst, src in loads:
                sp_.dma_start(dst[:], src).then_inc(weights_in, 16)
            for dst, src in late_loads:
                sp_.dma_start(dst[:], src).then_inc(late_weights_in, 16)
            sp_.wait_ge(weights_in, 16 * len(loads))
            sp_.wait_ge(arrived, 4)
            sp_.sem_clear(range(s[COUNTS[0]].num, s[COUNTS[-1]].num + 1))
            sp_.sem_clear(arrived)
            sp_.sem_inc(go, 1)

            def body(i, mamba, slots, ffn):
                waits = []
                if mamba:
                    sp_.dma_start(xres[:], tokens(x, i)).then_inc(s["xres_load"], 16)
                    sp_.wait_ge(s["pre_norm"], TT)
                    sp_.dma_start(xin[:], tokens(x, (i + 1) % BATCH)).then_inc(s["xin_load"], 16)
                    waits += ["xres_load", "xin_load"]
                if ffn:
                    sp_.wait_ge(s["out_norm"], TT)
                    sp_.dma_start(tokens(out, i - 2), acc.rearrange("p (i e) -> p i e", e=E)).then_inc(s["out_store"], 16)
                    waits += ["out_store"]
                if mamba:
                    if slots:
                        sp_.wait_ge(s["pnT_ready"], 2)
                    sp_.dma_start(ctxt[:], ctx_in[bass.ds(i, 1)].rearrange("a m e -> (a m) e")).then_inc(s["ctx_load"], 16)
                    waits += ["ctx_load"]
                for w in waits:
                    sp_.wait_ge(s[w], 16)
                sp_.wait_ge(arrived, 4)
                sp_.sem_clear(range(s[COUNTS[0]].num, s[COUNTS[-1]].num + 1))
                sp_.sem_clear(arrived)
                sp_.sem_inc(go, 1)

            iterations(sp_, body)

        @block.gpsimd
        def _(pool):
            pool.memset(ones[:], 1.0).then_inc(consts_done, 1)
            pool.memset(mhalf[:], -0.5).then_inc(consts_done, 1)
            pool.memset(rms_eps[:], RMS_EPS).then_inc(consts_done, 1)
            pool.memset(ident[:], 0.0).then_inc(consts_done, 1)
            pool.wait_ge(consts_done, 4)
            pool.affine_select(out=ident[:], in_=ident[:], compare_op=ALU.not_equal, fill=1.0, base=0,
                               pattern=[[-1, P]], channel_multiplier=1).then_inc(consts_done, 1)

            def rstd(name):
                pool.wait_ge(s[f"{name}_ve"], 1)
                pool.tensor_tensor(stats[name][3][:], stats[name][2][:], mhalf[:], ALU.pow).then_inc(s[f"{name}_rs"], 1)

            rstd("pre")
            meet(pool, 1)

            def slot_step(step, k=0, j=0):
                if (step, k) == ("ctx", 0):
                    pool.wait_ge(s["c_ve"], 1)
                    pool.tensor_tensor(small[:, 2:3], small[:, 1:2], mhalf[0:M, 0:1], ALU.pow).then_inc(s["c_rs"], 1)
                elif step == "cand":
                    pool.wait_ge(s["n_ready"], ET * (k + 1))
                    pool.tensor_tensor(nh, hT[:].rearrange("p a t -> p (a t)"), nn, ALU.subtract).then_inc(s["d_done"], 1)
                elif (step, k) == ("final", 1):
                    rstd("x2")
                elif step == "out_stats":
                    rstd("out")
                elif step == "next_stats":
                    rstd("pre")

            def body(i, mamba, slots, ffn):
                def filler(position):
                    take(position, slot_step, mamba, slots, ffn)

                if mamba:
                    pool.memset(upad[:, :, 0:KC - 1], 0.0).then_inc(s["upad_zero"], 1)
                for position in ("start", "norm", "u", "z", "x"):
                    filler(position)
                if mamba:
                    pool.wait_ge(s["conv_step"], (KC - 1) * DT)
                    pool.wait_ge(s["bc_split"], 5)
                    pool.wait_ge(s["pre_full"], 7 + DT)
                    pool.memset(d_a[:, :, :, 0:1], 0.0).then_inc(s["da_zero"], 1)
                    for c in range(DT):
                        pool.wait_ge(s["sp_ln"], c + 1)
                        pool.tensor_tensor(dt[:, c], dt[:, c], sp[:, c], ALU.add).then_inc(s["dt_ready"], 1)
                        pool.wait_ge(s["dt_ready"], c + 1)
                        pool.tensor_tensor(dtu[:, c], dt[:, c], u2[:, c], ALU.mult).then_inc(s["dtu_ready"], 1)
                filler("dt")
                for g in range(SLOTS):
                    if mamba and g < GROUPS:
                        q = g % PAIRS
                        pool.wait_ge(s["scan_done"], g + 1)
                        pool.wait_ge(s["cb_ready"], 2 * q + 2)
                        pool.tensor_tensor(h[:, g % HR], h[:, g % HR], cb[:, 2 * q:2 * q + 2], ALU.mult).then_inc(s["hc_done"], 1)
                    if mamba and chunk_end(g) is not None:
                        c = chunk_end(g)
                        pool.wait_ge(s["ypost_done"], c + 1)
                        pool.tensor_tensor(yv[:, c], yv[:, c], sz[:, c], ALU.mult).then_inc(s["yz_done"], 1)
                    filler(g)
                if mamba:
                    rstd("post")
                meet(pool, i + 2)

            iterations(pool, body)

        @block.tensor
        def _(pe):
            def merge_weights():
                pe.wait_ge(late_weights_in, 16 * len(late_loads))
                for e1 in range(ET):
                    for d in range(ET):
                        mm = pe.matmul(px[:, e1, 0:E], wk[:, d, e1 * P:(e1 + 1) * P], wq[:, d, :], start=(d == 0), stop=(d == ET - 1))
                mm.then_inc(setup_full, 1)
                for e1 in range(ET):
                    pe.wait_ge(setup_copied, e1 + 1)
                    for j in range(2):
                        for d in range(ET):
                            mm = pe.matmul(px[:, j, 0:384], wv[:, d, e1 * P:(e1 + 1) * P], wih[:, d, j * 384:(j + 1) * 384],
                                           start=(d == 0), stop=(d == ET - 1))
                    mm.then_inc(setup_full, 1)

            pe.wait_ge(weights_in, 16 * len(loads))
            meet(pe, 1)

            def slot_step(step, k=0, j=0):
                if step == "ctx":
                    if k == 1:
                        pe.wait_ge(s["c_norm"], 1)
                        for e in range(ET):
                            mm = pe.transpose(px[:, 0, e * M:(e + 1) * M], ctxt[:, e * P:(e + 1) * P], ident[0:M, 0:M])
                        mm.then_inc(s["x_full"], 1)
                    if k == 2:
                        pe.wait_ge(s["pnT_ready"], 2)
                        for e in range(ET):
                            for d in range(ET):
                                mm = pe.matmul(px[:, 1, e * M:(e + 1) * M], mqk[:, d, e * P:(e + 1) * P], pnT[:, d],
                                               start=(d == 0), stop=(d == ET - 1))
                        mm.then_inc(s["x_full"], 1)
                    if k == 3:
                        for j in range(2):
                            if j == 1:
                                pe.wait_ge(s["g_ready"], 2)
                            for d in range(ET):
                                mm = pe.matmul(px[0:M, j, 0:384], pnT[:, d], wvih[:, d, j * 384:(j + 1) * 384],
                                               start=(d == 0), stop=(d == ET - 1))
                            mm.then_inc(s["x_full"], 1)
                    return
                f0 = 4 + 10 * k
                if step == "norm":
                    pe.wait_ge(s["vw_ready"], 2)
                    if k:
                        pe.wait_ge(s["h_done"], k)
                        pe.wait_ge(s["v2_done"], 2 * k)
                    pe.wait_ge(s["sq_ready"], k + 1)
                    for e in range(ET):
                        pe.matmul(px[0:M, 1, :], gT[:, e], hT[:, e], start=(e == 0), stop=(e == ET - 1))
                        mm = pe.matmul(px[M:2 * M, 0, :], ones[:, 0:M], nn[:, e * L:(e + 1) * L], start=(e == 0), stop=(e == ET - 1))
                    mm.then_inc(s["x_full"], 1)
                elif step == "soft":
                    pe.wait_ge(s["an0_done"], k + 1)
                    pe.wait_ge(s["lnss_done"], k + 1)
                    pe.matmul(px[0:M, 0, :], ones[0:M, :], an[:], start=True, stop=True).then_inc(s["x_full"], 1)
                elif step == "gate":
                    b = (j + 1) % 2
                    if j == 0:
                        pe.wait_ge(s["sc_done"], k + 1)
                    elif j == 1:
                        pe.wait_ge(s["eps_done"], k + 1)
                    else:
                        pe.wait_ge(s["trz_ready"], 4 * k + j - 1)
                    for e in range(ET):
                        pe.matmul(px[:, b, :], whh[:, e, j * P:(j + 1) * P], hT[:, e], start=(e == 0), stop=False)
                    if j == 0:
                        pe.wait_ge(s["an_done"], k + 1)
                    pe.matmul(px[:, b, :], vw[:, j * P:(j + 1) * P], an[:], start=False, stop=True).then_inc(s["x_full"], 1)
                elif step == "cand_h":
                    b = (j + 1) % 2
                    pe.wait_ge(s["trz_ready"], 4 * k + 3 + j)
                    for e in range(ET):
                        mm = pe.matmul(px[:, b, :], whh[:, e, (4 + j) * P:(5 + j) * P], hT[:, e], start=(e == 0), stop=(e == ET - 1))
                    mm.then_inc(s["x_full"], 1)
                elif step == "cand_x":
                    b = (j + 1) % 2
                    pe.wait_ge(s["nh_ready"], ET * k + j + 1)
                    pe.matmul(px[:, b, :], vw[:, (4 + j) * P:(5 + j) * P], an[:], start=True, stop=True).then_inc(s["x_full"], 1)
                elif step == "up":
                    ffn_up(k)
                elif step == "final":
                    if k == 0:
                        pe.wait_ge(s["h_done"], NI)
                        pe.wait_ge(s["v2_done"], 2 * NI)
                        for i2 in range(TT):
                            for e in range(ET):
                                o = (i2 % 2) * E + e * P
                                mm = pe.transpose(px[:, i2 // 2, o:o + P], hT[:, e, i2 * P:(i2 + 1) * P], ident[:])
                        mm.then_inc(s["x_full"], 1)
                    if k == 2:
                        pe.wait_ge(s["x2_norm"], TT)
                        for e in range(ET):
                            for i2 in range(TT):
                                mm = pe.transpose(px[:, e, i2 * P:(i2 + 1) * P], x2[:, i2, e * P:(e + 1) * P], ident[:])
                            mm.then_inc(s["x_full"], 1)

            def pre_a():
                pe.wait_ge(s["pre_norm"], TT)
                for e in range(ET):
                    for i2 in range(TT):
                        mm = pe.transpose(pb[:, e, i2 * P:(i2 + 1) * P], xn[:, i2, e * P:(e + 1) * P], ident[:])
                    mm.then_inc(s["pre_full"], 1)

            def u_proj(c):
                pe.wait_ge(s["xnT_ready"], 2)
                for e in range(ET):
                    mm = pe.matmul(pb[:, (2 + c) % 4, :], w_in[:, e, c * P:(c + 1) * P], xnT[:, e], start=(e == 0), stop=(e == ET - 1))
                mm.then_inc(s["pre_full"], 1)

            def x_proj():
                pe.wait_ge(s["u_ready"], DT)
                for c in range(DT):
                    mm = pe.matmul(pb[0:3 * BC + DTR, 2, :], w_x[:, c], u2[:, c], start=(c == 0), stop=(c == DT - 1))
                mm.then_inc(s["pre_full"], 1)

            def dt_proj():
                pe.wait_ge(s["dtin_ready"], 1)
                for c in range(DT):
                    if c == 2:
                        pe.wait_ge(s["bc_split"], 2)
                    pe.matmul(pb[:, c, :], w_dt[:, c * P:(c + 1) * P], dtin, start=True, stop=True).then_inc(s["pre_full"], 1)

            def z_proj(c):
                if c >= 2:
                    pe.wait_ge(s["sz_ready"], c - 1)
                bank = py if c % 2 else pc
                for e in range(ET):
                    mm = pe.matmul(bank[:], w_in[:, e, (DT + c) * P:(DT + c + 1) * P], xnT[:, e], start=(e == 0), stop=(e == ET - 1))
                mm.then_inc(s["z_full"], 1)

            def ffn_up(f):
                if f < 2:
                    pe.wait_ge(s["x2T_ready"], 2)
                else:
                    pe.wait_ge(s["f_relu"], f - 1)
                for e in range(ET):
                    mm = pe.matmul(px[:, f % 2, :], w_fc[:, e, f * P:(f + 1) * P], x2T[:, e], start=(e == 0), stop=(e == ET - 1))
                mm.then_inc(s["f_full"], 1)

            def out_proj(c):
                for i2 in range(TT):
                    mm = pe.matmul(pb[:, i2, 0:E], yv[:, c, i2 * P:(i2 + 1) * P], w_out[:, c], start=(c == 0), stop=(c == DT - 1))
                    if c == DT - 1:
                        mm.then_inc(s["op_full"], 1)

            def ffn_down(i2):
                if i2 == 0:
                    pe.wait_ge(s["f_sq"], FT)
                for f in range(FT):
                    mm = pe.matmul(px[:, i2 // 2, (i2 % 2) * E:(i2 % 2 + 1) * E], hid[:, f, i2 * P:(i2 + 1) * P], w_pr[:, f],
                                   start=(f == 0), stop=(f == FT - 1))
                mm.then_inc(s["fd_full"], 1)

            def bcb(g):
                n = 2 * (g % PAIRS)
                if g < 2:
                    pe.wait_ge(s["sp_abs"], DT)
                    pe.wait_ge(s["bc_split"], 5)
                else:
                    pe.wait_ge(s["scan_done"], g - 1)
                for j in range(2):
                    mm = pe.matmul(pb[:, 2 * (g % 2) + j, :], sel[:, n + j:n + j + 1].to_broadcast([3 * BC, P]), bcs[:], start=True, stop=True)
                mm.then_inc(s["bcb_full"], 1)

            def cbm(n):
                if n:
                    pe.wait_ge(s["cb_ready"], n)
                else:
                    pe.wait_ge(s["sz_ready"], DT)
                pe.matmul(pc[:], sel[:, NS + n:NS + n + 1].to_broadcast([3 * BC, P]), bcs[:], start=True, stop=True).then_inc(s["cb_full"], 1)

            def hsum(g):
                c, q = g // PAIRS, g % PAIRS
                pe.wait_ge(s["hc_done"], g + 1)
                if q == 0 and c:
                    pe.wait_ge(s["yt_ready"], c)
                for j in range(2):
                    for i2 in range(TT):
                        cols_ = slice(i2 * P, (i2 + 1) * P)
                        mm = pe.matmul(py[:, cols_], h[:, g % HR, j, cols_], ident[:], is_transpose=True,
                                       start=(q == 0 and j == 0 and i2 == 0), stop=(q == PAIRS - 1 and j == 1), skip_group_check=True)
                mm.then_inc(s["hsum_done"], 1)

            def y_back(c):
                pe.wait_ge(s["yt_ready"], c + 1)
                for i2 in range(TT):
                    mm = pe.transpose(pc[:, i2 * P:(i2 + 1) * P], yv[:, c, i2 * P:(i2 + 1) * P], ident[:])
                mm.then_inc(s["yback_full"], 1)

            def body(i, mamba, slots, ffn):
                def filler(position):
                    take(position, slot_step, mamba, slots, ffn)

                filler("start")
                if mamba:
                    pre_a()
                filler("norm")
                if mamba:
                    for c in range(DT):
                        u_proj(c)
                filler("u")
                if mamba:
                    for c in range(DT):
                        z_proj(c)
                filler("z")
                if mamba:
                    x_proj()
                filler("x")
                if mamba:
                    dt_proj()
                filler("dt")
                for g in range(SLOTS):
                    if mamba:
                        if g == 0:
                            bcb(0)
                            cbm(0)
                            cbm(1)
                        if g + 1 < GROUPS:
                            bcb(g + 1)
                        if g + 1 < PAIRS:
                            cbm(2 * g + 2)
                            cbm(2 * g + 3)
                        if chunk_end(g) is not None:
                            y_back(chunk_end(g))
                        if LAG <= g < GROUPS + LAG:
                            hsum(g - LAG)
                        if g == MERGE_SLOT and not slots:
                            merge_weights()
                    filler(g)
                    if mamba and g == GROUPS + LAG - 1:
                        pe.wait_ge(s["scan_done"], GROUPS)
                        pe.wait_ge(s["yz_done"], DT - 1)
                        for c in range(DT - 1):
                            out_proj(c)
                if slots:
                    ffn_down(0)
                    ffn_down(1)
                if mamba:
                    pe.wait_ge(s["yz_done"], DT)
                    out_proj(DT - 1)
                if slots:
                    ffn_down(2)
                    ffn_down(3)
                if mamba:
                    pe.wait_ge(s["post_norm"], TT)
                    for e in range(ET):
                        for i2 in range(TT):
                            mm = pe.transpose(pb[:, e, i2 * P:(i2 + 1) * P], x1[:, i2, e * P:(e + 1) * P], ident[:])
                        mm.then_inc(s["post_full"], 1)
                meet(pe, i + 2)

            iterations(pe, body)

        @block.scalar
        def _(act):
            def merge_weights():
                act.wait_ge(setup_full, 1)
                act.activation(mqk[:], px[:, :, 0:E], ACT.Copy).then_inc(setup_copied, 1)
                for e1 in range(ET):
                    act.wait_ge(setup_full, 2 + e1)
                    act.activation(wvih[:, e1, :].rearrange("p (j n) -> p j n", n=384), px[:, :, 0:384], ACT.Copy).then_inc(setup_copied, 1)

            act.wait_ge(weights_in, 16 * len(loads))
            act.activation(neg_a[:], cols[:, COLS["A_log"]], ACT.Exp).then_inc(a_done, 1)
            meet(act, 1)

            def slot_step(step, k=0, j=0):
                if step == "ctx":
                    if k == 0:
                        act.activation(sc[:, 0:E], ctxt[:], ACT.Square, accum_out=small[:, 0:1]).then_inc(s["c_sq"], 1)
                    if k == 1:
                        act.wait_ge(s["x_full"], 1)
                        for e in range(ET):
                            act.activation(pnT[:, e], px[:, 0, e * M:(e + 1) * M], ACT.Copy, scale=col("input_w", e)).then_inc(s["pnT_ready"], 1)
                    if k == 2:
                        act.wait_ge(s["x_full"], 2)
                        for e in range(ET):
                            act.activation(gT[:, e], px[:, 1, e * M:(e + 1) * M], ACT.Copy, scale=g_scale[:, e:e + 1]).then_inc(s["g_ready"], 1)
                    if k == 3:
                        for j in range(2):
                            act.wait_ge(s["x_full"], 3 + j)
                            act.activation(vw[:, j * 384:(j + 1) * 384], px[0:M, j, 0:384], ACT.Copy).then_inc(s["vw_ready"], 1)
                    return
                f0 = 4 + 10 * k
                if step == "norm":
                    if k:
                        act.wait_ge(s["h_done"], k)
                    act.activation(nn, hT[:].rearrange("p a t -> p (a t)"), ACT.Square).then_inc(s["sq_ready"], 1)
                    act.wait_ge(s["x_full"], f0 + 1)
                    act.activation(rt[:], px[M:2 * M, 0, :], ACT.Ln, scale=1.0 / E, bias=rms_eps[M:2 * M, :]).then_inc(s["lnss_done"], 1)
                    act.wait_ge(s["lnss_done"], k + 1)
                    act.activation(rt[:], rt[:], ACT.Exp, scale=-0.5).then_inc(s["rsb_done"], 1)
                elif step == "score":
                    act.wait_ge(s["nmx_done"], k + 1)
                    act.activation(sc[:], sc[:], ACT.Exp, bias=small[:, 4:5], accum_out=small[:, 5:6]).then_inc(s["ex_done"], 1)
                elif step == "soft":
                    act.wait_ge(s["x_full"], f0 + 2)
                    act.activation(rt[:], px[0:M, 0, :], ACT.Ln, bias=rms_eps[0:M, :]).then_inc(s["lnv_done"], 1)
                    act.wait_ge(s["lnv_done"], k + 1)
                    act.activation(rt[:], rt[:], ACT.Exp, scale=-1.0).then_inc(s["rt_done"], 1)
                elif step == "gate":
                    act.wait_ge(s["x_full"], f0 + 3 + j)
                    act.activation(xs[:, j // 2, (j % 2) * L:(j % 2 + 1) * L], px[:, (j + 1) % 2, :], ACT.Tanh, scale=0.5,
                                   bias=half_b[:, j:j + 1]).then_inc(s["trz_ready"], 1)
                elif step == "cand_h":
                    act.wait_ge(s["x_full"], f0 + 7 + j)
                    act.activation(nh[:, j * L:(j + 1) * L], px[:, (j + 1) % 2, :], ACT.Identity, scale=0.5,
                                   bias=half_b[:, 4 + j:5 + j]).then_inc(s["nh_ready"], 1)
                elif step == "up":
                    act.wait_ge(s["f_full"], k + 1)
                    act.activation(hid[:, k], px[:, k % 2, :], ACT.Relu).then_inc(s["f_relu"], 1)
                    act.wait_ge(s["f_relu"], k + 1)
                    act.activation(hid[:, k], hid[:, k], ACT.Square).then_inc(s["f_sq"], 1)
                elif step == "cand":
                    for j in range(ET):
                        act.wait_ge(s["v2_done"], ET * k + j + 1)
                        act.activation(nn[:, j * L:(j + 1) * L], nh[:, j * L:(j + 1) * L], ACT.Tanh,
                                       bias=col("bih", 4 + j)).then_inc(s["n_ready"], 1)
                elif step == "final" and k == 3:
                    for e in range(ET):
                        act.wait_ge(s["x_full"], 4 + 10 * NI + 2 + e)
                        act.activation(x2T[:, e], px[:, e, :], ACT.Copy).then_inc(s["x2T_ready"], 1)

            def body(i, mamba, slots, ffn):
                def filler(position):
                    take(position, slot_step, mamba, slots, ffn)

                filler("start")
                if mamba:
                    for e in range(ET):
                        act.wait_ge(s["pre_full"], e + 1)
                        act.activation(xnT[:, e], pb[:, e, :], ACT.Identity, scale=col("ln_g", e), bias=col("ln_b", e)).then_inc(s["xnT_ready"], 1)
                filler("norm")
                if mamba:
                    act.wait_ge(s["upad_zero"], 1)
                    for j in range(DT):
                        act.wait_ge(s["pre_full"], 3 + j)
                        act.activation(upad[:, j, KC - 1:], pb[:, (2 + j) % 4, :], ACT.Copy)
                        act.activation(u2[:, j], pb[:, (2 + j) % 4, :], ACT.Identity, scale=col("conv_w", j * KC + KC - 1),
                                       bias=col("conv_b", j)).then_inc(s["uacc_ready"], 1)
                filler("u")
                if mamba:
                    for j in range(DT):
                        act.wait_ge(s["conv_step"], 6 * (j // 2) + 5 + j % 2)
                        if j >= 2:
                            act.wait_ge(s["u_ready"], j - 1)
                        act.activation(th[:, j % 2], u2[:, j], ACT.Tanh, scale=0.5).then_inc(s["uth_ready"], 1)
                    for j in range(DT):
                        act.wait_ge(s["z_full"], j + 1)
                        if j >= 2:
                            act.wait_ge(s["sz_ready"], j - 1)
                        act.activation(th[:, 2 + j % 2], (py if j % 2 else pc)[:], ACT.Tanh, scale=0.5).then_inc(s["zth_ready"], 1)
                filler("z")
                if mamba:
                    act.wait_ge(s["pre_full"], 7)
                    act.activation(dtin, pb[3 * BC:3 * BC + DTR, 2, :], ACT.Copy).then_inc(s["dtin_ready"], 1)
                filler("x")
                if mamba:
                    for c in range(DT):
                        act.wait_ge(s["pre_full"], 8 + c)
                        act.activation(dt[:, c], pb[:, c, :], ACT.Relu, bias=col("dt_bias", c))
                        act.activation(sp[:, c], pb[:, c, :], ACT.Abs, bias=col("dt_bias", c)).then_inc(s["sp_abs"], 1)
                    act.wait_ge(s["sp_abs"], DT)
                    act.activation(sp[:], sp[:], ACT.Exp, scale=-1.0).then_inc(s["sp_exp"], 1)
                    act.wait_ge(s["sp_exp"], 1)
                    for c in range(DT):
                        act.activation(sp[:, c], sp[:, c], ACT.Ln, bias=1.0).then_inc(s["sp_ln"], 1)

                filler("dt")

                def cb_copy(n):
                    act.wait_ge(s["cb_full"], n + 1)
                    act.activation(cb[:, n], pc[:], ACT.Copy).then_inc(s["cb_ready"], 1)

                def decay(g):
                    c, n = g // PAIRS, 2 * (g % PAIRS)
                    if g == 0:
                        act.wait_ge(s["da_zero"], 1)
                    if g % PAIRS == 0:
                        act.wait_ge(s["dt_ready"], c + 1)
                    if g >= 2:
                        act.wait_ge(s["scan_done"], g - 1)
                    for j in range(2):
                        ins = act.activation(d_a[:, g % 2, j, 1:], dt[:, c, 1:], ACT.Exp, scale=neg_a[:, c * NS + n + j:c * NS + n + j + 1])
                    ins.then_inc(s["da_ready"], 1)

                for g in range(SLOTS):
                    if mamba:
                        if g == 0:
                            decay(0)
                            cb_copy(0)
                            cb_copy(1)
                        if g + 1 < GROUPS:
                            decay(g + 1)
                        if g + 1 < PAIRS:
                            cb_copy(2 * g + 2)
                            cb_copy(2 * g + 3)
                        if g > LAG and (g - LAG) % PAIRS == PAIRS - 1:
                            c = (g - LAG) // PAIRS
                            act.wait_ge(s["hsum_done"], PAIRS * (c + 1))
                            act.wait_ge(s["dt_ready"], DT)
                            act.activation(yv[:, c], py[:], ACT.Copy).then_inc(s["yt_ready"], 1)
                        if g == MERGE_SLOT and not slots:
                            merge_weights()
                    filler(g)
                if mamba:
                    if slots:
                        act.wait_ge(s["x_full"], 4 + 10 * NI + 1)
                    for e in range(ET):
                        act.wait_ge(s["post_full"], e + 1)
                        act.activation(hT[:, e], pb[:, e, :], ACT.Copy).then_inc(s["hT_loaded"], 1)
                meet(act, i + 2)

            iterations(act, body)

        @block.vector
        def _(dve):
            dve.wait_ge(weights_in, 16 * len(loads))
            dve.wait_ge(a_done, 1)
            dve.wait_ge(consts_done, 5)
            dve.tensor_scalar(neg_a[:], neg_a[:], -1.0, None, ALU.mult)
            dve.tensor_tensor(half_b[:], cols[:, COLS["bih"]], cols[:, COLS["bhh"]], ALU.add).then_inc(params_done, 1)
            dve.wait_ge(params_done, 1)
            dve.tensor_copy(half_b[:, 4:6], cols[:, COLS["bhh"].start + 4:COLS["bhh"].start + 6]).then_inc(params_done, 1)
            dve.wait_ge(params_done, 2)
            dve.tensor_scalar(half_b[:], half_b[:], 0.5, None, ALU.mult)
            dve.tensor_scalar(half_d[:], cols[:, COLS["D"]], 0.5, None, ALU.mult)
            dve.tensor_scalar(g_scale[:], cols[:, COLS["slot_w"]], SCALE, None, ALU.mult)
            dve.tensor_scalar(w_x[:, :, 3 * BC:], w_x[:, :, 3 * BC:], 0.5, None, ALU.mult)
            for r in range(3):
                o = r * BC
                dve.tensor_scalar(w_x[:, :, o:o + NS], w_x[:, :, o:o + NS], 0.25, None, ALU.mult)
                dve.tensor_scalar(w_x[:, :, o + NS:o + BC], w_x[:, :, o + NS:o + BC], 0.5, None, ALU.mult)
            dve.tensor_tensor(sel32[:], ident[0:3 * BC, 0:BC], ident[0:3 * BC, BC:2 * BC], ALU.add).then_inc(params_done, 1)
            dve.wait_ge(params_done, 3)
            dve.tensor_tensor(sel32[:], sel32[:], ident[0:3 * BC, 2 * BC:3 * BC], ALU.add).then_inc(params_done, 1)
            dve.wait_ge(params_done, 4)
            dve.tensor_copy(sel[:], sel32[:])

            def norm_stats(name, src):
                st, mv, var, _ = stats[name]
                for i2 in range(TT):
                    dve.bn_stats(st[:, i2], src[:, i2]).then_inc(s[f"{name}_stat"], 1)
                dve.wait_ge(s[f"{name}_stat"], TT)
                for i2 in range(TT):
                    dve.bn_aggr(mv[:, i2], st[:, i2]).then_inc(s[f"{name}_aggr"], 1)
                dve.wait_ge(s[f"{name}_aggr"], TT)
                dve.tensor_scalar(var[:], mv[:, :, 1], LN_EPS, None, ALU.add).then_inc(s[f"{name}_ve"], 1)

            def norm_apply(name, src, dst):
                _, mv, _, rstd = stats[name]
                if name != "pre":
                    dve.wait_ge(s[f"{name}_rs"], 1)
                for i2 in range(TT):
                    dve.tensor_scalar(dst[:, i2], src[:, i2], mv[:, i2, 0:1], rstd[:, i2:i2 + 1], ALU.subtract,
                                      ALU.mult).then_inc(s[f"{name}_norm"], 1)

            norm_stats("pre", xin)
            meet(dve, 1)

            def slot_step(step, k=0, j=0):
                if step == "spike":
                    spike(k)
                elif step == "out_stats":
                    dve.wait_ge(s["out_res"], 1)
                    norm_stats("out", memv)
                elif step == "out_norm":
                    norm_apply("out", memv, accv)
                elif step == "next_stats":
                    dve.wait_ge(s["xin_load"], 16)
                    norm_stats("pre", xin)
                if step == "ctx":
                    if k == 0:
                        dve.wait_ge(s["c_sq"], 1)
                        dve.tensor_scalar(small[:, 1:2], small[:, 0:1], 1.0 / E, RMS_EPS, ALU.mult, ALU.add).then_inc(s["c_ve"], 1)
                    if k == 1:
                        dve.wait_ge(s["c_rs"], 1)
                        dve.tensor_scalar(ctxt[:], ctxt[:], small[:, 2:3], None, ALU.mult).then_inc(s["c_norm"], 1)
                    return
                f0 = 4 + 10 * k
                if step == "score":
                    dve.wait_ge(s["rsb_done"], k + 1)
                    dve.tensor_tensor(sc[:], px[0:M, 1, :], rt[:], ALU.mult).then_inc(s["sc_done"], 1)
                    dve.wait_ge(s["sc_done"], k + 1)
                    dve.tensor_reduce(small[:, 3:4], sc[:], AX.X, ALU.max).then_inc(s["mx_done"], 1)
                    dve.wait_ge(s["mx_done"], k + 1)
                    dve.tensor_scalar(small[:, 4:5], small[:, 3:4], -1.0, None, ALU.mult).then_inc(s["nmx_done"], 1)
                elif step == "soft":
                    dve.wait_ge(s["ex_done"], k + 1)
                    dve.reciprocal(small[:, 6:7], small[:, 5:6]).then_inc(s["rz_done"], 1)
                    dve.wait_ge(s["rz_done"], k + 1)
                    dve.tensor_scalar(an[:], sc[:], small[:, 6:7], None, ALU.mult).then_inc(s["an0_done"], 1)
                elif step == "renorm":
                    dve.wait_ge(s["rt_done"], k + 1)
                    dve.scalar_tensor_tensor(sc[:], px[0:M, 0, :], RMS_EPS, rt[:], ALU.add, ALU.mult).then_inc(s["eps_done"], 1)
                    dve.wait_ge(s["eps_done"], k + 1)
                    dve.scalar_tensor_tensor(rt[:], sc[:], 2.0, rt[:], ALU.subtract, ALU.mult, reverse0=True).then_inc(s["newton_done"], 1)
                    dve.wait_ge(s["newton_done"], k + 1)
                    dve.tensor_tensor(an[:], an[:], rt[:], ALU.mult).then_inc(s["an_done"], 1)
                elif step == "cand_x":
                    if j == 0:
                        dve.wait_ge(s["nh_ready"], ET * (k + 1))
                        dve.scalar_tensor_tensor(nh, tr, 1.0, nh, ALU.add, ALU.mult).then_inc(s["v1_done"], 1)
                        dve.wait_ge(s["v1_done"], k + 1)
                    dve.wait_ge(s["x_full"], f0 + 9 + j)
                    dve.tensor_tensor(nh[:, j * L:(j + 1) * L], nh[:, j * L:(j + 1) * L], px[:, (j + 1) % 2, :],
                                      ALU.add).then_inc(s["v2_done"], 1)
                elif step == "update":
                    dve.wait_ge(s["d_done"], k + 1)
                    dve.scalar_tensor_tensor(nh, tz, 1.0, nh, ALU.add, ALU.mult).then_inc(s["e_done"], 1)
                    dve.wait_ge(s["e_done"], k + 1)
                    dve.scalar_tensor_tensor(hT[:].rearrange("p a t -> p (a t)"), nh, 0.5, nn, ALU.mult, ALU.add).then_inc(s["h_done"], 1)
                elif step == "final":
                    x2v = x2[:].rearrange("p i e -> p (i e)")
                    if k == 0:
                        dve.wait_ge(s["x_full"], 4 + 10 * NI + 1)
                        dve.tensor_tensor(x2v, px[:].rearrange("p a t -> p (a t)"), x1[:].rearrange("p i e -> p (i e)"),
                                          ALU.add).then_inc(s["xs_done"], 1)
                        dve.wait_ge(s["xs_done"], 1)
                        norm_stats("x2", x2)
                    if k == 1:
                        norm_apply("x2", x2, x2)

            def spike(n):
                if n == 0:
                    dve.tensor_scalar(cnt, y_sb, THRESHOLD, None, ALU.is_gt).then_inc(s["spike"], 1)
                    return
                dve.wait_ge(s["spike"], n)
                if n == SPIKE_OPS - 1:
                    dve.scalar_tensor_tensor(mem, cnt, 1.0 / STEPS, x2[:].rearrange("p i e -> p (i e)"), ALU.mult,
                                             ALU.add).then_inc(s["out_res"], 1)
                    return
                t, k = divmod(n - 1, 3)
                old = mem if t else y_sb
                if k == 0:
                    ins = dve.scalar_tensor_tensor(acc, old, BETA, y_sb, ALU.mult, ALU.add)
                if k == 1:
                    ins = dve.scalar_tensor_tensor(mem, old, THRESHOLD, acc, ALU.is_gt, ALU.subtract, reverse1=True)
                if k == 2:
                    ins = dve.scalar_tensor_tensor(cnt, mem, THRESHOLD, cnt, ALU.is_gt, ALU.add)
                ins.then_inc(s["spike"], 1)

            memv = mem.rearrange("p (i e) -> p i e", e=E)
            accv = acc.rearrange("p (i e) -> p i e", e=E)

            def body(i, mamba, slots, ffn):
                def filler(position):
                    take(position, slot_step, mamba, slots, ffn)

                filler("start")
                if mamba:
                    norm_apply("pre", xin, xn)
                filler("norm")
                if mamba:
                    for c0 in (0, 2):
                        for t in range(KC - 1):
                            for c in (c0, c0 + 1):
                                if t == 0:
                                    dve.wait_ge(s["uacc_ready"], c + 1)
                                else:
                                    dve.wait_ge(s["conv_step"], 3 * c0 + 2 * t + c - c0 - 1)
                                dve.scalar_tensor_tensor(u2[:, c], upad[:, c, t:t + L], col("conv_w", c * KC + t), u2[:, c],
                                                         ALU.mult, ALU.add).then_inc(s["conv_step"], 1)
                filler("u")
                if mamba:
                    for c in range(DT):
                        dve.wait_ge(s["uth_ready"], c + 1)
                        dve.scalar_tensor_tensor(u2[:, c], th[:, c % 2], 1.0, u2[:, c], ALU.add, ALU.mult).then_inc(s["u_ready"], 1)
                    for c in range(DT):
                        dve.wait_ge(s["zth_ready"], c + 1)
                        dve.scalar_tensor_tensor(sz[:, c], th[:, 2 + c % 2], 1.0, (py if c % 2 else pc)[:], ALU.add, ALU.mult).then_inc(s["sz_ready"], 1)
                filler("z")
                if mamba:
                    dve.wait_ge(s["pre_full"], 7)
                    dve.tensor_copy(bcs[:], pb[0:3 * BC, 2, :]).then_inc(s["bc_split"], 1)
                    dve.wait_ge(s["bc_split"], 1)
                    dve.tensor_tensor(bcr, pb[0:3 * BC, 2, :], bcs[:], ALU.subtract).then_inc(s["bc_split"], 1)
                    dve.wait_ge(s["bc_split"], 2)
                    dve.tensor_copy(bcs[BC:2 * BC], bcr[BC:2 * BC]).then_inc(s["bc_split"], 1)
                    dve.tensor_copy(bcs[2 * BC:3 * BC], bcr[2 * BC:3 * BC]).then_inc(s["bc_split"], 1)
                    dve.wait_ge(s["bc_split"], 4)
                    dve.tensor_tensor(bcs[2 * BC:3 * BC], bcr[2 * BC:3 * BC], bcs[2 * BC:3 * BC], ALU.subtract).then_inc(s["bc_split"], 1)

                filler("x")
                filler("dt")

                def mul(g):
                    c, b = g // PAIRS, 2 * (g % 2)
                    dve.wait_ge(s["bcb_full"], g + 1)
                    if g % PAIRS == 0:
                        dve.wait_ge(s["dtu_ready"], c + 1)
                    dve.tensor_tensor(pb[:, b:b + 2, :], pb[:, b:b + 2, :], dtu[:, c:c + 1, :].to_broadcast([P, 2, L]),
                                      ALU.mult).then_inc(s["mul_done"], 1)

                def scan(g):
                    b = 2 * (g % 2)
                    dve.wait_ge(s["da_ready"], g + 1)
                    dve.wait_ge(s["mul_done"], g + 1)
                    if g >= HR:
                        dve.wait_ge(s["hsum_done"], g - HR + 1)
                    dve.tensor_tensor_scan(h2[:, g % HR], d_a2[:, g % 2], pb[:, b:b + 2, :].rearrange("p a t -> p (a t)"), 0.0,
                                           ALU.mult, ALU.add).then_inc(s["scan_done"], 1)

                for g in range(SLOTS):
                    if mamba:
                        if g == 0:
                            mul(0)
                        if g + 1 < GROUPS:
                            mul(g + 1)
                        if g < GROUPS:
                            scan(g)
                        if chunk_end(g) is not None:
                            c = chunk_end(g)
                            dve.wait_ge(s["yback_full"], c + 1)
                            dve.scalar_tensor_tensor(yv[:, c], u2[:, c], half_d[:, c:c + 1], pc[:], ALU.mult, ALU.add).then_inc(s["ypost_done"], 1)
                        if g == MERGE_SLOT and not slots:
                            dve.wait_ge(late_weights_in, 16 * len(late_loads))
                            dve.tensor_scalar(w_out[:], w_out[:], 0.5, None, ALU.mult)
                    filler(g)
                if mamba:
                    dve.wait_ge(s["xres_load"], 16)
                    for i2 in range(TT):
                        dve.wait_ge(s["op_full"], i2 + 1)
                        dve.scalar_tensor_tensor(xres[:, i2], xres[:, i2], 2.0, pb[:, i2, 0:E], ALU.mult, ALU.add).then_inc(s["res_done"], 1)
                    dve.wait_ge(s["res_done"], TT)
                    norm_stats("post", xres)
                    norm_apply("post", xres, x1)
                if slots:
                    dve.wait_ge(s["fd_full"], TT)
                    dve.tensor_copy(y_sb, px[:].rearrange("p a t -> p (a t)")).then_inc(s["y_copied"], 1)
                meet(dve, i + 2)

            iterations(dve, body)


def kernel(**inputs):
    import numpy as np
    import concourse.bacc as bacc
    from concourse.bass_utils import run_bass_kernel_spmd

    def rows(a, n):
        a = np.asarray(a).reshape(n, P, -1)
        return a.transpose(1, 0, 2).reshape(P, -1)

    w = {k: np.asarray(v) for k, v in inputs.items()}
    w_x = w["L0_attn_W_x"].T
    cols = np.concatenate([rows(w["L0_attn_conv_w"], DT), rows(w["L0_attn_conv_b"], DT), rows(w["L0_attn_dt_bias"], DT),
                           rows(w["L0_attn_A_log"], DT), rows(w["L0_attn_D"], DT), rows(w["L0_xattn_gru_bih"], 6),
                           rows(w["L0_xattn_gru_bhh"], 6), rows(w["L0_xattn_slot_norm_w"], ET),
                           rows(w["L0_xattn_input_norm_w"], ET), rows(w["L0_attn_ln_g"], ET), rows(w["L0_attn_ln_b"], ET)], axis=1)
    arrays = {
        "x_in": w["x"], "ctx_in": w["ctx_1024"], "cols_in": cols,
        "w_inT_in": w["L0_attn_W_in"].T,
        "w_xT_in": np.concatenate([w_x[:, DTR:]] * 3 + [w_x[:, :DTR]], axis=1),
        "w_dtT_in": w["L0_attn_W_dt"].T, "w_outT_in": w["L0_attn_W_out"].T,
        "wq_in": w["L0_xattn_Wq"], "wk_in": w["L0_xattn_Wk"], "wv_in": w["L0_xattn_Wv"],
        "wihT_in": w["L0_xattn_gru_wih"].T, "whhT_in": w["L0_xattn_gru_whh"].T,
        "w_fcT_in": w["L0_ffn_W_fc"].T, "w_prT_in": w["L0_ffn_W_proj"].T,
    }
    arrays = {k: np.ascontiguousarray(v) for k, v in arrays.items()}
    nc = bacc.Bacc("TRN2", target_bir_lowering=False, num_devices=1)
    args = [nc.dram_tensor(k, a.shape, F32, kind="ExternalInput").ap() for k, a in arrays.items()]
    out = nc.dram_tensor("x_out", (BATCH, L, E), F32, kind="ExternalOutput").ap()
    decoder_layer(nc, *args, out)
    r = run_bass_kernel_spmd(nc, [arrays], core_ids=[0])
    return r.results[0]["x_out"]
```

```python
from contextlib import ExitStack

import concourse.bass as bass
from concourse import mybir

F32 = mybir.dt.float32
BF16 = mybir.dt.bfloat16
ALU = mybir.AluOpType
ACT = mybir.ActivationFunctionType
AX = mybir.AxisListType

P = 128
BATCH, L, E = 8, 512, 256
DIN, NS, DTR, KC = 512, 16, 16, 4
M = 64
F = 4 * E
NI = 3
ET, DT, FT, TT = E // P, DIN // P, F // P, L // P
BC = 2 * NS
PAIRS = NS // 2
GROUPS = DT * PAIRS
LAG = 2
SCALE = float(E) ** -0.5
LN_EPS, RMS_EPS = 1e-5, 1e-6
BETA, THRESHOLD, STEPS = 0.9, 1.0, 5
HR = 3
LN_EXP = "natural_log_exp_and_others"

COLS = {}
_at = 0
for _name, _n in (("conv_w", DT * KC), ("conv_b", DT), ("dt_bias", DT), ("A_log", DT * NS), ("D", DT),
                  ("bih", 6), ("bhh", 6), ("slot_w", ET), ("input_w", ET), ("ln_g", ET), ("ln_b", ET)):
    COLS[_name] = slice(_at, _at + _n)
    _at += _n
NCOLS = _at

COUNTS = """
next_stat next_aggr next_ve next_rs next_norm next_full xnT_ready u_full pre_full upad_zero uacc_ready conv_step uth_ready u_ready
z_full zth_ready sz_ready bc_split dtin_ready sp_abs sp_exp sp_ln dt_ready dtu_ready da_zero yt_ready yback_full
cb_full cb_ready bcb_full da_ready mul_done scan_done hc_done hsum_done ypost_done yz_done
op_half op_full res_done post_stat post_aggr post_ve post_rs post_norm post_full hT_loaded
c_sq c_ve c_rs c_norm x_full pnT_ready g_ready vw_ready sq_ready lnss_done rsb_done sc_done mx_done nmx_done ex_done
rz_done an0_done lnv_done rt_done eps_done newton_done an_done trz_ready nh_ready v1_done v2_done n_ready d_done e_done h_done
xs_done x2_stat x2_aggr x2_ve x2_rs x2_norm x2T_ready
f_full unit_read f_sq fd_full early_spike spike x2_kept out_res out_stat out_aggr out_ve out_rs out_norm
xin_load xres_load ctx_load out_store
""".split()


def decoder_layer(nc, x, ctx_in, cols_d, w_inT, w_xT, w_dtT, w_outT, wq_d, wk_d, wv_d, wihT, whhT, w_fcT, w_prT, out):
    with ExitStack() as ctx:
        def sb(name, shape, dt=F32):
            return ctx.enter_context(nc.sbuf_tensor(name, shape, dt))

        def ps(name, shape):
            return ctx.enter_context(nc.psum_tensor(name, shape, F32))

        w_in = sb("w_in", [P, ET, 2 * DIN])
        w_x = sb("w_x", [P, DT, DTR + 3 * BC])
        w_dt = sb("w_dt", [3 * BC + DTR, DIN])[3 * BC:, :]
        w_out = sb("w_out", [P, DT, E])
        whh = sb("whh", [P, ET, 3 * E])
        wvih = sb("wvih", [P, ET, 3 * E])
        mqk = sb("mqk", [P, ET, E])
        w_fc = sb("w_fc", [P, ET, F])
        w_pr = sb("w_pr", [P, FT, E])
        cols = sb("cols", [P, NCOLS])
        neg_a = sb("neg_a", [P, DT * NS])
        half_b = sb("half_b", [P, 6])
        half_d = sb("half_d", [P, DT])
        g_scale = sb("g_scale", [P, ET])
        ident = sb("ident", [P, P])
        ones = sb("ones", [P, M])
        mhalf = sb("mhalf", [P, TT])
        rms_eps = sb("rms_eps", [P, 1])
        sel32 = sb("sel32", [3 * BC, BC])
        sel = sb("sel", [3 * BC, BC], BF16)

        reg_a = sb("reg_a", [P, 2060 + HR * 1024])
        reg_y = sb("reg_y", [P, DT, L])
        upad = reg_a[:, 0:2060].rearrange("p (c t) -> p c t", c=DT)
        d_a = reg_a[:, 0:2048].rearrange("p (s n t) -> p s n t", s=2, n=2)
        h = reg_a[:, 2060:].rearrange("p (s n t) -> p s n t", s=HR, n=2)
        h2 = reg_a[:, 2060:].rearrange("p (s t) -> p s t", s=HR)
        d_a2 = reg_a[:, 0:2048].rearrange("p (s t) -> p s t", s=2)
        bcr = reg_a[0:3 * BC, 0:L]
        dtin = reg_a[3 * BC:3 * BC + DTR, L:2 * L]
        xn = reg_y[:, 0:2, :].rearrange("p a (b e) -> p (a b) e", e=E)
        xnT = reg_y[:, 2:4, :]
        sp = reg_y
        yv = reg_y

        xin = sb("xin", [P, TT, E])
        u2 = sb("u2", [P, DT, L])
        sz = sb("sz", [P, DT, L])
        dt = sb("dt", [P, DT, L])
        dtu = sb("dtu", [P, DT, L])
        cb = sb("cb", [P, NS, L])
        bcs = sb("bcs", [3 * BC, L], BF16)
        x1 = sb("x1", [P, TT, E])
        hT = sb("hT", [P, ET, L])
        x2 = sb("x2", [P, TT, E])
        x2_old = sb("x2_old", [P, TT, E])
        x2T = sb("x2T", [P, ET, L])
        xs = sb("xs", [P, 4, 2 * L])
        tr, tz, nh, nn = (xs[:, j, :] for j in range(4))
        y_sb = sb("y_sb", [P, 2 * L])[:]
        reg_m = sb("reg_m", [P, 4 * L])
        mem, acc = reg_m[:, 0:2 * L], reg_m[:, 2 * L:4 * L]
        hid = reg_m[:].rearrange("p (f t) -> p f t", t=L)
        xres = tr.rearrange("p (i e) -> p i e", e=E)
        cnt = sb("cnt", [P, 2 * L], BF16)[:]
        sc = sb("sc", [M, L])
        an = sb("an", [M, L])
        rt = sb("rt", [M, L])
        gT = sb("gT", [P, ET, M])
        pnT = sb("pnT", [P, ET, M])
        vw = sb("vw", [M, 3 * E])
        ctxt = sb("ctxt", [M, E])
        small = sb("small", [M, 8])
        stats = {n: (sb(f"{n}_st", [P, TT, 6]), sb(f"{n}_mv", [P, TT, 2]), sb(f"{n}_var", [P, TT]),
                     sb(f"{n}_rstd", [P, TT])) for n in ("next", "post", "x2", "out")}

        pb = ps("pb", [P, 4, L])
        py = ps("py", [P, L])
        pc = ps("pc", [P, L])
        px = ps("px", [P, 2, L])

        def c_bank(n):
            return py[:] if n in (1, 3) else pc[:]

        def c_reads_before(n):
            return {2: 1, 3: 2, 4: 3}.get(n, n)

        z_banks = (pc[:], py[:], pb[:, 0, :], pb[:, 1, :])

        s = {n: ctx.enter_context(nc.semaphore(n)) for n in COUNTS}
        first_x_in = ctx.enter_context(nc.semaphore("first_x_in"))
        late_weights_in = ctx.enter_context(nc.semaphore("late_weights_in"))
        weights_in = ctx.enter_context(nc.semaphore("weights_in"))
        consts_done = ctx.enter_context(nc.semaphore("consts_done"))
        params_done = ctx.enter_context(nc.semaphore("params_done"))
        setup_full = ctx.enter_context(nc.semaphore("setup_full"))
        setup_copied = ctx.enter_context(nc.semaphore("setup_copied"))
        a_done = ctx.enter_context(nc.semaphore("a_done"))
        arrived = ctx.enter_context(nc.semaphore("arrived"))
        resumed = ctx.enter_context(nc.semaphore("resumed"))
        go = ctx.enter_context(nc.semaphore("go"))

        def col(name, j):
            return cols[:, COLS[name].start + j:COLS[name].start + j + 1]

        def tokens(dram, b):
            return dram[bass.ds(b, 1)].rearrange("a (i p) e -> (a p) i e", p=P)

        wq, wk, wv = (xs[:, 0:2, :].rearrange("p a (b t) -> p (a b) t", b=2)[:, j, :].rearrange("p (k n) -> p k n", k=ET) for j in range(3))
        wih = xs[:, 2:4, :].rearrange("p a t -> p (a t)")[:, 0:ET * 3 * E].rearrange("p (k n) -> p k n", k=ET)

        def k_rows(w):
            return w.rearrange("(k p) n -> p k n", p=P)

        loads = [(cols, cols_d), (w_in, k_rows(w_inT)), (w_x, k_rows(w_xT)), (w_dt, w_dtT)]
        late_loads = [(w_out, k_rows(w_outT)), (wq, k_rows(wq_d)), (wk, k_rows(wk_d)), (wv, k_rows(wv_d)),
                      (wih, k_rows(wihT)), (whh, k_rows(whhT)), (w_fc, k_rows(w_fcT)), (w_pr, k_rows(w_prT))]
        MERGE_SLOT = 10

        block = ctx.enter_context(nc.Block())

        def meet(eng, nxt):
            eng.drain().then_inc(arrived, 1)
            eng.wait_ge(go, nxt)
            eng.sem_inc(resumed, 1)

        def iterations(eng, body):
            for i in range(3):
                body(i, True, i >= 1, i >= 2, False)
            with eng.Fori(3, BATCH) as i:
                body(i, True, True, True, True)
            for i in range(BATCH, BATCH + 3):
                body(i, False, i == BATCH, i <= BATCH + 1, True)

        SLOTS = GROUPS + LAG + 1
        SPIKE_OPS = 2 + 3 * (STEPS - 1)
        EARLY_SPIKES = 6
        UPS = FT // 2

        def chunk_end(g):
            c, r = divmod(g - LAG, PAIRS)
            return c - 1 if 1 <= c <= DT and r == 0 else None

        plan = {}

        def place(position, *steps):
            plan.setdefault(position, []).extend(steps)

        def place_round(k, positions):
            parts = ([("sq", k)], [("norm", k)], [("score", k)], [("gate_h", k, 0)], [("soft", k)], [("colsum", k)], [("renorm", k)],
                     [("gate_x", k, 0), ("gate_h", k, 1), ("gate_x", k, 1)], [("gate_h", k, 2), ("gate_x", k, 2)],
                     [("gate_h", k, 3), ("gate_x", k, 3), ("cand_h", k, 0)],
                     [("cand_h", k, 1), ("cand_x", k, 0), ("cand_x", k, 1)], [("cand", k)], [("update", k)])
            for position, part in zip(positions, parts):
                place(position, *part)

        place("start", ("ctx", 0), ("ctx_norm",))
        place("z", ("ctx", 1), ("ctx", 2))
        place("u", ("ctx", 3))
        for position, n in zip((33, 33, 'end', 'end', 'end', 'post', 'x', 'x', 'dt', 'dt', 'dt', 0, 1, 2), range(SPIKE_OPS)):
            place(position, ("early_spike" if n < EARLY_SPIKES else "spike", n))
        units = [(half, *unit) for half in range(2) for unit in [("up", f) for f in range(UPS)] + [("down", i2) for i2 in range(TT)]]
        for position, (half, name, j) in zip((10, 11, 12, 13, 19, 19, 19, 20, 21, 23, 24, 25, 29, 30, 31, 31), units):
            place(position, (name, half, j))
        place_round(0, ('u', 'x', 'dt', 'dt', 0, 1, 2, 4, 5, 6, 7, 7, 8))
        place_round(1, (9, 9, 10, 11, 11, 11, 12, 13, 15, 16, 17, 18, 19))
        place_round(2, (19, 20, 21, 21, 22, 23, 24, 25, 26, 28, 29, 29, 30))
        place(1, ("sp_exp",))
        place(2, ("sp_ln",))
        for position, c in zip((3, 6, 6), range(1, DT)):
            place(position, ("dt", c))
        place(4, ("out_stats",))
        place(8, ("out_norm",))
        place(26, ("keep_x2",))
        place(27, ("next_stats",))
        place(31, ("final", 0))
        place(33, ("final", 1))
        place("end", ("final", 2), ("final", 3))
        SPIKE_STEPS = ("spike", "out_stats", "out_norm")
        FFN_STEPS = ("up", "down", "keep_x2", "early_spike")
        MAMBA_STEPS = ("next_stats", "sp_exp", "sp_ln", "dt")

        def reads_before(half, name, j):
            return half * (UPS + TT // 2) + (j if name == "up" else UPS + j // 2)

        def unit_bank(half, name, j, mamba):
            return py[:] if not mamba and reads_before(half, name, j) % 2 else pc[:]

        def reads_before_slot(g):
            return sum(step[0] == "up" or (step[0] == "down" and step[2] % 2 == 1)
                       for position in range(g) for step in plan.get(position, ()))

        def chunks_back(g):
            return sum(chunk_end(position) is not None for position in range(g + 1))

        def take(position, slot_step, mamba, slots, ffn, spikes):
            for step in plan.get(position, ()):
                kind = step[0]
                if (spikes if kind in SPIKE_STEPS else ffn if kind in FFN_STEPS else mamba if kind in MAMBA_STEPS else slots):
                    if kind in ("up", "down"):
                        slot_step(*step, back=chunks_back(position) if mamba else 0, spikes=spikes, mamba=mamba)
                    else:
                        slot_step(*step, spikes=spikes, ffn=ffn)

        @block.sync
        def _(sp_):
            sp_.dma_start(xin[:], tokens(x, 0)).then_inc(first_x_in, 16)
            for dst, src in loads:
                sp_.dma_start(dst[:], src).then_inc(weights_in, 16)
            for dst, src in late_loads:
                sp_.dma_start(dst[:], src).then_inc(late_weights_in, 16)
            sp_.wait_ge(first_x_in, 16)
            sp_.wait_ge(weights_in, 16 * len(loads))
            sp_.wait_ge(arrived, 4)
            sp_.sem_clear(range(s[COUNTS[0]].num, s[COUNTS[-1]].num + 1))
            sp_.sem_clear(arrived)
            sp_.sem_inc(go, 1)

            def body(i, mamba, slots, ffn, spikes):
                waits = []
                if mamba:
                    sp_.dma_start(xin[:], tokens(x, (i + 1) % BATCH)).then_inc(s["xin_load"], 16)
                    if slots:
                        sp_.wait_ge(s["pnT_ready"], 2)
                    sp_.dma_start(ctxt[:], ctx_in[bass.ds(i, 1)].rearrange("a m e -> (a m) e")).then_inc(s["ctx_load"], 16)
                    waits += ["xin_load", "ctx_load"]
                if spikes:
                    sp_.wait_ge(s["out_norm"], TT)
                    sp_.dma_start(tokens(out, i - 3), acc.rearrange("p (i e) -> p i e", e=E)).then_inc(s["out_store"], 16)
                    waits += ["out_store"]
                if mamba:
                    if slots:
                        sp_.wait_ge(s["h_done"], NI)
                    else:
                        sp_.wait_ge(s["scan_done"], GROUPS)
                    sp_.dma_start(xres, tokens(x, i)).then_inc(s["xres_load"], 16)
                    waits += ["xres_load"]
                for w in waits:
                    sp_.wait_ge(s[w], 16)
                sp_.wait_ge(arrived, 4)
                sp_.sem_clear(range(s[COUNTS[0]].num, s[COUNTS[-1]].num + 1))
                sp_.sem_clear(arrived)
                sp_.sem_inc(go, 1)

            iterations(sp_, body)

        @block.gpsimd
        def _(pool):
            pool.memset(ones[:], 1.0).then_inc(consts_done, 1)
            pool.memset(mhalf[:], -0.5).then_inc(consts_done, 1)
            pool.memset(rms_eps[:], RMS_EPS).then_inc(consts_done, 1)
            pool.memset(ident[:], 0.0).then_inc(consts_done, 1)
            pool.wait_ge(consts_done, 4)
            pool.affine_select(out=ident[:], in_=ident[:], compare_op=ALU.not_equal, fill=1.0, base=0,
                               pattern=[[-1, P]], channel_multiplier=1).then_inc(consts_done, 1)

            def rstd(name):
                pool.wait_ge(s[f"{name}_ve"], 1)
                pool.tensor_tensor(stats[name][3][:], stats[name][2][:], mhalf[:], ALU.pow).then_inc(s[f"{name}_rs"], 1)

            pool.memset(upad[:, :, 0:KC - 1], 0.0).then_inc(s["upad_zero"], 1)
            rstd("next")
            meet(pool, 1)

            def slot_step(step, k=0, j=0, back=0, ffn=False, spikes=False, mamba=False):
                if (step, k) == ("ctx", 0):
                    pool.wait_ge(s["c_ve"], 1)
                    pool.tensor_tensor(small[:, 2:3], small[:, 1:2], mhalf[0:M, 0:1], ALU.pow).then_inc(s["c_rs"], 1)
                elif step == "cand":
                    pool.wait_ge(s["n_ready"], ET * (k + 1))
                    pool.tensor_tensor(nh, hT[:].rearrange("p a t -> p (a t)"), nn, ALU.subtract).then_inc(s["d_done"], 1)
                elif (step, k) == ("final", 1):
                    rstd("x2")
                elif step == "out_stats":
                    rstd("out")
                elif step == "next_stats":
                    rstd("next")
                elif step == "dt":
                    step_size(k)

            def step_size(c):
                pool.wait_ge(s["sp_ln"], c + 1)
                pool.tensor_tensor(dt[:, c], dt[:, c], sp[:, c], ALU.add).then_inc(s["dt_ready"], 1)
                pool.wait_ge(s["dt_ready"], c + 1)
                pool.tensor_tensor(dtu[:, c], dt[:, c], u2[:, c], ALU.mult).then_inc(s["dtu_ready"], 1)

            def body(i, mamba, slots, ffn, spikes):
                def filler(position):
                    take(position, slot_step, mamba, slots, ffn, spikes)

                for position in ("start", "z", "u", "x"):
                    filler(position)
                if mamba:
                    pool.wait_ge(s["conv_step"], (KC - 1) * DT)
                    pool.wait_ge(s["bc_split"], 5)
                    pool.wait_ge(s["pre_full"], DT + 1)
                    pool.memset(d_a[:, :, :, 0:1], 0.0).then_inc(s["da_zero"], 1)
                    step_size(0)
                filler("dt")
                for g in range(SLOTS):
                    if mamba and g < GROUPS:
                        q = g % PAIRS
                        pool.wait_ge(s["scan_done"], g + 1)
                        pool.wait_ge(s["cb_ready"], 2 * q + 2)
                        pool.tensor_tensor(h[:, g % HR], h[:, g % HR], cb[:, 2 * q:2 * q + 2], ALU.mult).then_inc(s["hc_done"], 1)
                    if mamba and chunk_end(g) is not None:
                        c = chunk_end(g)
                        pool.wait_ge(s["ypost_done"], c + 1)
                        pool.tensor_tensor(yv[:, c], yv[:, c], sz[:, c], ALU.mult).then_inc(s["yz_done"], 1)
                    filler(g)
                if mamba:
                    pool.wait_ge(s["scan_done"], GROUPS)
                    pool.memset(upad[:, :, 0:KC - 1], 0.0).then_inc(s["upad_zero"], 1)
                    rstd("post")
                meet(pool, i + 2)

            iterations(pool, body)

        @block.tensor
        def _(pe):
            def merge_weights():
                pe.wait_ge(late_weights_in, 16 * len(late_loads))
                for e1 in range(ET):
                    for d in range(ET):
                        mm = pe.matmul(px[:, e1, 0:E], wk[:, d, e1 * P:(e1 + 1) * P], wq[:, d, :], start=(d == 0), stop=(d == ET - 1))
                mm.then_inc(setup_full, 1)
                for e1 in range(ET):
                    pe.wait_ge(setup_copied, e1 + 1)
                    for j in range(2):
                        for d in range(ET):
                            mm = pe.matmul(px[:, j, 0:384], wv[:, d, e1 * P:(e1 + 1) * P], wih[:, d, j * 384:(j + 1) * 384],
                                           start=(d == 0), stop=(d == ET - 1))
                    mm.then_inc(setup_full, 1)

            def next_transposes():
                pe.wait_ge(s["next_norm"], TT)
                for e in range(ET):
                    for i2 in range(TT):
                        mm = pe.transpose((pc, py)[e][:, i2 * P:(i2 + 1) * P], xn[:, i2, e * P:(e + 1) * P], ident[:])
                    mm.then_inc(s["next_full"], 1)

            def u_proj(c):
                if c == 0:
                    pe.wait_ge(s["xnT_ready"], ET)
                for e in range(ET):
                    mm = pe.matmul(pb[:, c, :], w_in[:, e, c * P:(c + 1) * P], xnT[:, e], start=(e == 0), stop=(e == ET - 1))
                mm.then_inc(s["u_full"], 1)

            pe.wait_ge(consts_done, 5)
            next_transposes()
            pe.wait_ge(weights_in, 16 * len(loads))
            for c in range(DT):
                u_proj(c)
            meet(pe, 1)

            def slot_step(step, k=0, j=0, back=0, ffn=False, spikes=False, mamba=False):
                if step == "ctx":
                    if k == 1:
                        pe.wait_ge(s["c_norm"], 1)
                        for e in range(ET):
                            mm = pe.transpose(px[:, 0, e * M:(e + 1) * M], ctxt[:, e * P:(e + 1) * P], ident[0:M, 0:M])
                        mm.then_inc(s["x_full"], 1)
                    if k == 2:
                        pe.wait_ge(s["pnT_ready"], 2)
                        for e in range(ET):
                            for d in range(ET):
                                mm = pe.matmul(px[:, 1, e * M:(e + 1) * M], mqk[:, d, e * P:(e + 1) * P], pnT[:, d],
                                               start=(d == 0), stop=(d == ET - 1))
                        mm.then_inc(s["x_full"], 1)
                    if k == 3:
                        for j in range(2):
                            if j == 1:
                                pe.wait_ge(s["g_ready"], 2)
                            for d in range(ET):
                                mm = pe.matmul(px[0:M, j, 0:384], pnT[:, d], wvih[:, d, j * 384:(j + 1) * 384],
                                               start=(d == 0), stop=(d == ET - 1))
                            mm.then_inc(s["x_full"], 1)
                    return
                f0 = 4 + 10 * k
                if step == "norm":
                    pe.wait_ge(s["vw_ready"], 2)
                    if k:
                        pe.wait_ge(s["h_done"], k)
                        pe.wait_ge(s["v2_done"], 2 * k)
                    pe.wait_ge(s["sq_ready"], k + 1)
                    for e in range(ET):
                        pe.matmul(px[0:M, 0, :], gT[:, e], hT[:, e], start=(e == 0), stop=(e == ET - 1))
                        mm = pe.matmul(px[M:2 * M, 0, :], ones[:, 0:M], nn[:, e * L:(e + 1) * L], start=(e == 0), stop=(e == ET - 1))
                    mm.then_inc(s["x_full"], 1)
                elif step == "colsum":
                    pe.wait_ge(s["sc_done"], k + 1)
                    pe.wait_ge(s["lnss_done"], k + 1)
                    pe.wait_ge(s["an0_done"], k + 1)
                    pe.matmul(px[0:M, 0, :], ones[0:M, :], an[:], start=True, stop=True).then_inc(s["x_full"], 1)
                elif step == "gate_h":
                    b = (j + 1) % 2
                    if j == 1:
                        pe.wait_ge(s["eps_done"], k + 1)
                    elif j > 1:
                        pe.wait_ge(s["trz_ready"], 4 * k + j - 1)
                    for e in range(ET):
                        pe.matmul(px[:, b, :], whh[:, e, j * P:(j + 1) * P], hT[:, e], start=(e == 0), stop=False)
                elif step == "gate_x":
                    if j == 0:
                        pe.wait_ge(s["an_done"], k + 1)
                    pe.matmul(px[:, (j + 1) % 2, :], vw[:, j * P:(j + 1) * P], an[:], start=False, stop=True).then_inc(s["x_full"], 1)
                elif step == "cand_h":
                    b = (j + 1) % 2
                    pe.wait_ge(s["trz_ready"], 4 * k + 3 + j)
                    for e in range(ET):
                        mm = pe.matmul(px[:, b, :], whh[:, e, (4 + j) * P:(5 + j) * P], hT[:, e], start=(e == 0), stop=(e == ET - 1))
                    mm.then_inc(s["x_full"], 1)
                elif step == "cand_x":
                    b = (j + 1) % 2
                    pe.wait_ge(s["nh_ready"], ET * k + j + 1)
                    pe.matmul(px[:, b, :], vw[:, (4 + j) * P:(5 + j) * P], an[:], start=True, stop=True).then_inc(s["x_full"], 1)
                elif step == "up":
                    ffn_up(k, j, back, mamba)
                elif step == "down":
                    ffn_down(k, j, back, mamba)
                elif step == "final":
                    if k == 0:
                        pe.wait_ge(s["h_done"], NI)
                        pe.wait_ge(s["v2_done"], 2 * NI)
                        for i2 in range(TT):
                            for e in range(ET):
                                o = (i2 % 2) * E + e * P
                                mm = pe.transpose(px[:, i2 // 2, o:o + P], hT[:, e, i2 * P:(i2 + 1) * P], ident[:])
                        mm.then_inc(s["x_full"], 1)
                    if k == 2:
                        pe.wait_ge(s["x2_norm"], TT)
                        for e in range(ET):
                            for i2 in range(TT):
                                mm = pe.transpose(px[:, e, i2 * P:(i2 + 1) * P], x2[:, i2, e * P:(e + 1) * P], ident[:])
                            mm.then_inc(s["x_full"], 1)

            def x_proj():
                pe.wait_ge(s["u_ready"], DT)
                for c in range(DT):
                    mm = pe.matmul(pb[0:3 * BC + DTR, 2, :], w_x[:, c], u2[:, c], start=(c == 0), stop=(c == DT - 1))
                mm.then_inc(s["pre_full"], 1)

            def dt_proj():
                pe.wait_ge(s["dtin_ready"], 1)
                for c in range(DT):
                    if c == 2:
                        pe.wait_ge(s["bc_split"], 2)
                    pe.matmul(pb[:, c, :], w_dt[:, c * P:(c + 1) * P], dtin, start=True, stop=True).then_inc(s["pre_full"], 1)

            def z_proj(c):
                for e in range(ET):
                    mm = pe.matmul(z_banks[c], w_in[:, e, (DT + c) * P:(DT + c + 1) * P], xnT[:, e], start=(e == 0), stop=(e == ET - 1))
                mm.then_inc(s["z_full"], 1)

            def out_proj(c):
                for i2 in range(TT):
                    mm = pe.matmul(pb[:, i2, 0:E], yv[:, c, i2 * P:(i2 + 1) * P], w_out[:, c], start=(c == 0), stop=(c == DT - 1))
                    if c == DT - 1:
                        mm.then_inc(s["op_full"], 1)
                if c == 1:
                    mm.then_inc(s["op_half"], 1)

            def unit_start(half, name, j, back, mamba):
                reads = reads_before(half, name, j) if mamba else reads_before(half, name, j) - 1
                if mamba and half == 0 and name == "up" and j == 0:
                    pe.wait_ge(s["cb_ready"], NS)
                if reads > 0:
                    pe.wait_ge(s["unit_read"], reads)
                if back:
                    pe.wait_ge(s["ypost_done"], back)

            def ffn_up(half, j, back, mamba):
                unit_start(half, "up", j, back, mamba)
                f = half * UPS + j
                for e in range(ET):
                    mm = pe.matmul(unit_bank(half, "up", j, mamba), w_fc[:, e, f * P:(f + 1) * P], x2T[:, e], start=(e == 0), stop=(e == ET - 1))
                mm.then_inc(s["f_full"], 1)

            def ffn_down(half, i2, back, mamba):
                unit_start(half, "down", i2, back, mamba)
                pe.wait_ge(s["f_sq"], UPS * (half + 1))
                bank = unit_bank(half, "down", i2, mamba)
                for j in range(UPS):
                    mm = pe.matmul(bank[:, (i2 % 2) * E:(i2 % 2 + 1) * E], hid[:, j, i2 * P:(i2 + 1) * P], w_pr[:, half * UPS + j],
                                   start=(j == 0), stop=(j == UPS - 1))
                mm.then_inc(s["fd_full"], 1)

            def bcb(g):
                n = 2 * (g % PAIRS)
                if g < 2:
                    pe.wait_ge(s["sp_abs"], 2 * g + 2)
                    pe.wait_ge(s["bc_split"], 5)
                else:
                    pe.wait_ge(s["scan_done"], g - 1)
                for j in range(2):
                    mm = pe.matmul(pb[:, 2 * (g % 2) + j, :], sel[:, n + j:n + j + 1].to_broadcast([3 * BC, P]), bcs[:], start=True, stop=True)
                mm.then_inc(s["bcb_full"], 1)

            def cbm(n):
                if n < 2:
                    pe.wait_ge(s["sz_ready"], DT)
                else:
                    pe.wait_ge(s["cb_ready"], c_reads_before(n))
                pe.matmul(c_bank(n), sel[:, NS + n:NS + n + 1].to_broadcast([3 * BC, P]), bcs[:], start=True, stop=True).then_inc(s["cb_full"], 1)

            def hsum(g):
                c, q = g // PAIRS, g % PAIRS
                pe.wait_ge(s["hc_done"], g + 1)
                if q == 0 and c:
                    pe.wait_ge(s["yt_ready"], c)
                for j in range(2):
                    for i2 in range(TT):
                        cols_ = slice(i2 * P, (i2 + 1) * P)
                        mm = pe.matmul(py[:, cols_], h[:, g % HR, j, cols_], ident[:], is_transpose=True,
                                       start=(q == 0 and j == 0 and i2 == 0), stop=(q == PAIRS - 1 and j == 1), skip_group_check=True)
                mm.then_inc(s["hsum_done"], 1)

            def y_back(c, reads):
                if reads:
                    pe.wait_ge(s["unit_read"], reads)
                pe.wait_ge(s["yt_ready"], c + 1)
                for i2 in range(TT):
                    mm = pe.transpose(pc[:, i2 * P:(i2 + 1) * P], yv[:, c, i2 * P:(i2 + 1) * P], ident[:])
                mm.then_inc(s["yback_full"], 1)

            def body(i, mamba, slots, ffn, spikes):
                def filler(position):
                    take(position, slot_step, mamba, slots, ffn, spikes)

                filler("start")
                if mamba:
                    for c in range(DT):
                        z_proj(c)
                filler("z")
                filler("u")
                if mamba:
                    x_proj()
                filler("x")
                if mamba:
                    pe.wait_ge(s["sz_ready"], DT)
                    dt_proj()
                filler("dt")
                for g in range(SLOTS):
                    if mamba:
                        if g == 0:
                            bcb(0)
                        if g + 1 < GROUPS:
                            bcb(g + 1)
                        if g == 0:
                            cbm(0)
                            cbm(1)
                        if g + 1 < PAIRS:
                            cbm(2 * g + 2)
                        if chunk_end(g) is not None:
                            y_back(chunk_end(g), reads_before_slot(g) if ffn else 0)
                        if LAG <= g < GROUPS + LAG:
                            hsum(g - LAG)
                        if g + 1 < PAIRS:
                            cbm(2 * g + 3)
                        if g == MERGE_SLOT and not slots:
                            merge_weights()
                    filler(g)
                if mamba:
                    pe.wait_ge(s["scan_done"], GROUPS)
                    pe.wait_ge(s["yz_done"], DT - 1)
                    for c in range(DT - 1):
                        out_proj(c)
                filler("end")
                if mamba:
                    pe.wait_ge(s["yz_done"], DT)
                    out_proj(DT - 1)
                if mamba:
                    next_transposes()
                    pe.wait_ge(s["res_done"], TT)
                    u_proj(0)
                    u_proj(1)
                    pe.wait_ge(s["post_norm"], TT)
                    if slots:
                        pe.wait_ge(s["x2T_ready"], ET)
                    for e in range(ET):
                        for i2 in range(TT):
                            mm = pe.transpose(px[:, e, i2 * P:(i2 + 1) * P], x1[:, i2, e * P:(e + 1) * P], ident[:])
                        mm.then_inc(s["post_full"], 1)
                    u_proj(2)
                    u_proj(3)
                meet(pe, i + 2)

            iterations(pe, body)

        @block.scalar
        def _(act):
            def merge_weights():
                act.wait_ge(setup_full, 1)
                act.activation(mqk[:], px[:, :, 0:E], ACT.Copy).then_inc(setup_copied, 1)
                for e1 in range(ET):
                    act.wait_ge(setup_full, 2 + e1)
                    act.activation(wvih[:, e1, :].rearrange("p (j n) -> p j n", n=384), px[:, :, 0:384], ACT.Copy).then_inc(setup_copied, 1)

            act.wait_ge(weights_in, 16 * len(loads))
            act.activation(neg_a[:], cols[:, COLS["A_log"]], ACT.Exp).then_inc(a_done, 1)

            def next_copies():
                for e in range(ET):
                    act.wait_ge(s["next_full"], e + 1)
                    act.activation(xnT[:, e], (pc, py)[e][:], ACT.Identity, scale=col("ln_g", e), bias=col("ln_b", e)).then_inc(s["xnT_ready"], 1)

            def u_copies(j):
                act.wait_ge(s["u_full"], j + 1)
                act.activation(upad[:, j, KC - 1:], pb[:, j, :], ACT.Copy)
                act.activation(u2[:, j], pb[:, j, :], ACT.Identity, scale=col("conv_w", j * KC + KC - 1),
                               bias=col("conv_b", j)).then_inc(s["uacc_ready"], 1)

            next_copies()
            act.wait_ge(s["upad_zero"], 1)
            for j in range(DT):
                u_copies(j)
            meet(act, 1)

            def slot_step(step, k=0, j=0, back=0, ffn=False, spikes=False, mamba=False):
                if step == "ctx":
                    if k == 0:
                        act.activation(sc[:, 0:E], ctxt[:], ACT.Square, accum_out=small[:, 0:1]).then_inc(s["c_sq"], 1)
                    if k == 1:
                        act.wait_ge(s["x_full"], 1)
                        for e in range(ET):
                            act.activation(pnT[:, e], px[:, 0, e * M:(e + 1) * M], ACT.Copy, scale=col("input_w", e)).then_inc(s["pnT_ready"], 1)
                    if k == 2:
                        act.wait_ge(s["x_full"], 2)
                        for e in range(ET):
                            act.activation(gT[:, e], px[:, 1, e * M:(e + 1) * M], ACT.Copy, scale=g_scale[:, e:e + 1]).then_inc(s["g_ready"], 1)
                    if k == 3:
                        for j in range(2):
                            act.wait_ge(s["x_full"], 3 + j)
                            act.activation(vw[:, j * 384:(j + 1) * 384], px[0:M, j, 0:384], ACT.Copy).then_inc(s["vw_ready"], 1)
                    return
                f0 = 4 + 10 * k
                if step == "sq":
                    if k:
                        act.wait_ge(s["h_done"], k)
                    act.activation(nn, hT[:].rearrange("p a t -> p (a t)"), ACT.Square).then_inc(s["sq_ready"], 1)
                elif step == "norm":
                    if k:
                        act.preload_act_table_set(LN_EXP)
                    act.wait_ge(s["x_full"], f0 + 1)
                    act.activation(rt[:], px[M:2 * M, 0, :], ACT.Ln, scale=1.0 / E, bias=rms_eps[M:2 * M, :]).then_inc(s["lnss_done"], 1)
                    act.wait_ge(s["lnss_done"], k + 1)
                    act.activation(rt[:], rt[:], ACT.Exp, scale=-0.5).then_inc(s["rsb_done"], 1)
                elif step == "score":
                    act.wait_ge(s["nmx_done"], k + 1)
                    act.activation(sc[:], sc[:], ACT.Exp, bias=small[:, 4:5], accum_out=small[:, 5:6]).then_inc(s["ex_done"], 1)
                elif step == "colsum":
                    act.wait_ge(s["x_full"], f0 + 2)
                    act.activation(rt[:], px[0:M, 0, :], ACT.Ln, bias=rms_eps[0:M, :]).then_inc(s["lnv_done"], 1)
                    act.wait_ge(s["lnv_done"], k + 1)
                    act.activation(rt[:], rt[:], ACT.Exp, scale=-1.0).then_inc(s["rt_done"], 1)
                elif step == "gate_x":
                    act.wait_ge(s["x_full"], f0 + 3 + j)
                    act.activation(xs[:, j // 2, (j % 2) * L:(j % 2 + 1) * L], px[:, (j + 1) % 2, :], ACT.Tanh, scale=0.5,
                                   bias=half_b[:, j:j + 1]).then_inc(s["trz_ready"], 1)
                elif step == "cand_h":
                    act.wait_ge(s["x_full"], f0 + 7 + j)
                    act.activation(nh[:, j * L:(j + 1) * L], px[:, (j + 1) % 2, :], ACT.Identity, scale=0.5,
                                   bias=half_b[:, 4 + j:5 + j]).then_inc(s["nh_ready"], 1)
                elif step == "up":
                    if spikes and k == 0 and j == 0:
                        act.wait_ge(s["out_norm"], TT)
                    if spikes and k == 0 and j == 2:
                        act.wait_ge(s["out_store"], 16)
                    act.wait_ge(s["f_full"], UPS * k + j + 1)
                    act.activation(hid[:, j], unit_bank(k, step, j, mamba), ACT.Relu).then_inc(s["unit_read"], 1)
                    act.wait_ge(s["unit_read"], reads_before(k, "up", j) + 1)
                    act.activation(hid[:, j], hid[:, j], ACT.Square).then_inc(s["f_sq"], 1)
                elif step == "down" and k == 0 and j % 2:
                    act.wait_ge(s["fd_full"], j + 1)
                    act.activation(y_sb[:, (j // 2) * L:(j // 2 + 1) * L], unit_bank(k, step, j, mamba), ACT.Copy).then_inc(s["unit_read"], 1)
                elif step == "keep_x2":
                    if spikes:
                        act.wait_ge(s["out_res"], 1)
                    act.activation(x2_old[:], x2[:], ACT.Copy).then_inc(s["x2_kept"], 1)
                elif step == "sp_exp":
                    act.activation(sp[:, 1:], sp[:, 1:], ACT.Exp, scale=-1.0).then_inc(s["sp_exp"], 1)
                elif step == "sp_ln":
                    act.wait_ge(s["sp_exp"], 2)
                    for c in range(1, DT):
                        act.activation(sp[:, c], sp[:, c], ACT.Ln, bias=1.0).then_inc(s["sp_ln"], 1)
                elif step == "cand":
                    for j in range(ET):
                        act.wait_ge(s["v2_done"], ET * k + j + 1)
                        act.activation(nn[:, j * L:(j + 1) * L], nh[:, j * L:(j + 1) * L], ACT.Tanh,
                                       bias=col("bih", 4 + j)).then_inc(s["n_ready"], 1)
                elif step == "final" and k == 3:
                    for e in range(ET):
                        act.wait_ge(s["x_full"], 4 + 10 * NI + 2 + e)
                        act.activation(x2T[:, e], px[:, e, :], ACT.Copy).then_inc(s["x2T_ready"], 1)

            def body(i, mamba, slots, ffn, spikes):
                def filler(position):
                    take(position, slot_step, mamba, slots, ffn, spikes)

                filler("start")
                def u_tanh(j):
                    act.wait_ge(s["conv_step"], 6 * (j // 2) + 5 + j % 2)
                    act.activation(dtu[:, j], u2[:, j], ACT.Tanh, scale=0.5).then_inc(s["uth_ready"], 1)

                def z_tanh(j):
                    act.wait_ge(s["z_full"], j + 1)
                    act.activation(sz[:, j], z_banks[j], ACT.Tanh, scale=0.5).then_inc(s["zth_ready"], 1)

                def softplus_parts(c):
                    act.wait_ge(s["pre_full"], 2 + c)
                    act.activation(dt[:, c], pb[:, c, :], ACT.Relu, bias=col("dt_bias", c))
                    act.activation(sp[:, c], pb[:, c, :], ACT.Abs, bias=col("dt_bias", c)).then_inc(s["sp_abs"], 1)

                if mamba:
                    z_tanh(0)
                    z_tanh(1)
                    z_tanh(2)
                    u_tanh(0)
                    u_tanh(1)
                    z_tanh(3)
                filler("z")
                if mamba:
                    u_tanh(2)
                    u_tanh(3)
                filler("u")
                if mamba or slots:
                    act.preload_act_table_set(LN_EXP)
                if mamba:
                    act.wait_ge(s["pre_full"], 1)
                    act.activation(dtin, pb[3 * BC:3 * BC + DTR, 2, :], ACT.Copy).then_inc(s["dtin_ready"], 1)
                filler("x")
                if mamba:
                    softplus_parts(0)
                    act.wait_ge(s["sp_abs"], 1)
                    act.activation(sp[:, 0], sp[:, 0], ACT.Exp, scale=-1.0).then_inc(s["sp_exp"], 1)
                    act.wait_ge(s["sp_exp"], 1)
                    act.activation(sp[:, 0], sp[:, 0], ACT.Ln, bias=1.0).then_inc(s["sp_ln"], 1)
                    for c in range(1, DT):
                        softplus_parts(c)
                filler("dt")

                def cb_copy(n):
                    act.wait_ge(s["cb_full"], n + 1)
                    act.activation(cb[:, n], c_bank(n), ACT.Copy).then_inc(s["cb_ready"], 1)

                def decay(g):
                    c, n = g // PAIRS, 2 * (g % PAIRS)
                    if g == 0:
                        act.wait_ge(s["da_zero"], 1)
                    if g % PAIRS == 0:
                        act.wait_ge(s["dt_ready"], c + 1)
                    if g >= 2:
                        act.wait_ge(s["scan_done"], g - 1)
                    for j in range(2):
                        ins = act.activation(d_a[:, g % 2, j, 1:], dt[:, c, 1:], ACT.Exp, scale=neg_a[:, c * NS + n + j:c * NS + n + j + 1])
                    ins.then_inc(s["da_ready"], 1)

                for g in range(SLOTS):
                    if mamba:
                        if g == 0:
                            decay(0)
                            cb_copy(0)
                            cb_copy(1)
                        if g + 1 < PAIRS:
                            cb_copy(2 * g + 2)
                        if g + 1 < GROUPS:
                            decay(g + 1)
                        if g + 1 < PAIRS:
                            cb_copy(2 * g + 3)
                        if g > LAG and (g - LAG) % PAIRS == PAIRS - 1:
                            c = (g - LAG) // PAIRS
                            act.wait_ge(s["hsum_done"], PAIRS * (c + 1))
                            act.wait_ge(s["dt_ready"], DT)
                            act.activation(yv[:, c], py[:], ACT.Copy).then_inc(s["yt_ready"], 1)
                        if g == MERGE_SLOT and not slots:
                            merge_weights()
                    filler(g)
                filler("end")
                if mamba:
                    next_copies()
                    act.wait_ge(s["upad_zero"], 1)
                    u_copies(0)
                    u_copies(1)
                    if slots:
                        act.wait_ge(s["x_full"], 4 + 10 * NI + 1)
                    for e in range(ET):
                        act.wait_ge(s["post_full"], e + 1)
                        act.activation(hT[:, e], px[:, e, :], ACT.Copy).then_inc(s["hT_loaded"], 1)
                    u_copies(2)
                    u_copies(3)
                meet(act, i + 2)

            iterations(act, body)

        @block.vector
        def _(dve):
            def norm_stats(name, src):
                st, mv, var, _ = stats[name]
                for i2 in range(TT):
                    dve.bn_stats(st[:, i2], src[:, i2]).then_inc(s[f"{name}_stat"], 1)
                dve.wait_ge(s[f"{name}_stat"], TT)
                for i2 in range(TT):
                    dve.bn_aggr(mv[:, i2], st[:, i2]).then_inc(s[f"{name}_aggr"], 1)
                dve.wait_ge(s[f"{name}_aggr"], TT)
                dve.tensor_scalar(var[:], mv[:, :, 1], LN_EPS, None, ALU.add).then_inc(s[f"{name}_ve"], 1)

            def norm_apply(name, src, dst):
                _, mv, _, rstd = stats[name]
                dve.wait_ge(s[f"{name}_rs"], 1)
                for i2 in range(TT):
                    dve.tensor_scalar(dst[:, i2], src[:, i2], mv[:, i2, 0:1], rstd[:, i2:i2 + 1], ALU.subtract,
                                      ALU.mult).then_inc(s[f"{name}_norm"], 1)

            dve.wait_ge(first_x_in, 16)
            norm_stats("next", xin)
            norm_apply("next", xin, xn)
            dve.wait_ge(weights_in, 16 * len(loads))
            dve.wait_ge(a_done, 1)
            dve.wait_ge(consts_done, 5)
            dve.tensor_scalar(neg_a[:], neg_a[:], -1.0, None, ALU.mult)
            dve.tensor_tensor(half_b[:], cols[:, COLS["bih"]], cols[:, COLS["bhh"]], ALU.add).then_inc(params_done, 1)
            dve.wait_ge(params_done, 1)
            dve.tensor_copy(half_b[:, 4:6], cols[:, COLS["bhh"].start + 4:COLS["bhh"].start + 6]).then_inc(params_done, 1)
            dve.wait_ge(params_done, 2)
            dve.tensor_scalar(half_b[:], half_b[:], 0.5, None, ALU.mult)
            dve.tensor_scalar(half_d[:], cols[:, COLS["D"]], 0.5, None, ALU.mult)
            dve.tensor_scalar(g_scale[:], cols[:, COLS["slot_w"]], SCALE, None, ALU.mult)
            dve.tensor_scalar(w_x[:, :, 3 * BC:], w_x[:, :, 3 * BC:], 0.5, None, ALU.mult)
            for r in range(3):
                o = r * BC
                dve.tensor_scalar(w_x[:, :, o:o + NS], w_x[:, :, o:o + NS], 0.25, None, ALU.mult)
                dve.tensor_scalar(w_x[:, :, o + NS:o + BC], w_x[:, :, o + NS:o + BC], 0.5, None, ALU.mult)
            dve.tensor_tensor(sel32[:], ident[0:3 * BC, 0:BC], ident[0:3 * BC, BC:2 * BC], ALU.add).then_inc(params_done, 1)
            dve.wait_ge(params_done, 3)
            dve.tensor_tensor(sel32[:], sel32[:], ident[0:3 * BC, 2 * BC:3 * BC], ALU.add).then_inc(params_done, 1)
            dve.wait_ge(params_done, 4)
            dve.tensor_copy(sel[:], sel32[:])
            meet(dve, 1)

            def slot_step(step, k=0, j=0, back=0, ffn=False, spikes=False, mamba=False):
                if step in ("spike", "early_spike"):
                    spike(k)
                elif step == "out_stats":
                    dve.wait_ge(s["out_res"], 1)
                    norm_stats("out", memv)
                elif step == "out_norm":
                    norm_apply("out", memv, accv)
                elif step == "ctx_norm":
                    dve.wait_ge(s["c_rs"], 1)
                    dve.tensor_scalar(ctxt[:], ctxt[:], small[:, 2:3], None, ALU.mult).then_inc(s["c_norm"], 1)
                elif step == "down" and k == 1 and j % 2:
                    half = y_sb[:, (j // 2) * L:(j // 2 + 1) * L]
                    dve.wait_ge(s["unit_read"], reads_before(k, step, j))
                    dve.wait_ge(s["fd_full"], TT + j + 1)
                    dve.tensor_tensor(half, half, unit_bank(k, step, j, mamba), ALU.add).then_inc(s["unit_read"], 1)
                elif step == "next_stats":
                    dve.wait_ge(s["xin_load"], 16)
                    norm_stats("next", xin)
                if step == "ctx":
                    if k == 0:
                        dve.wait_ge(s["c_sq"], 1)
                        dve.tensor_scalar(small[:, 1:2], small[:, 0:1], 1.0 / E, RMS_EPS, ALU.mult, ALU.add).then_inc(s["c_ve"], 1)
                    return
                f0 = 4 + 10 * k
                if step == "score":
                    dve.wait_ge(s["rsb_done"], k + 1)
                    dve.tensor_tensor(sc[:], px[0:M, 0, :], rt[:], ALU.mult).then_inc(s["sc_done"], 1)
                    dve.wait_ge(s["sc_done"], k + 1)
                    dve.tensor_reduce(small[:, 3:4], sc[:], AX.X, ALU.max).then_inc(s["mx_done"], 1)
                    dve.wait_ge(s["mx_done"], k + 1)
                    dve.tensor_scalar(small[:, 4:5], small[:, 3:4], -1.0, None, ALU.mult).then_inc(s["nmx_done"], 1)
                elif step == "soft":
                    dve.wait_ge(s["ex_done"], k + 1)
                    dve.reciprocal(small[:, 6:7], small[:, 5:6]).then_inc(s["rz_done"], 1)
                    dve.wait_ge(s["rz_done"], k + 1)
                    dve.tensor_scalar(an[:], sc[:], small[:, 6:7], None, ALU.mult).then_inc(s["an0_done"], 1)
                elif step == "renorm":
                    dve.wait_ge(s["rt_done"], k + 1)
                    dve.scalar_tensor_tensor(sc[:], px[0:M, 0, :], RMS_EPS, rt[:], ALU.add, ALU.mult).then_inc(s["eps_done"], 1)
                    dve.wait_ge(s["eps_done"], k + 1)
                    dve.scalar_tensor_tensor(rt[:], sc[:], 2.0, rt[:], ALU.subtract, ALU.mult, reverse0=True).then_inc(s["newton_done"], 1)
                    dve.wait_ge(s["newton_done"], k + 1)
                    dve.tensor_tensor(an[:], an[:], rt[:], ALU.mult).then_inc(s["an_done"], 1)
                elif step == "cand":
                    dve.wait_ge(s["nh_ready"], ET * (k + 1))
                    dve.scalar_tensor_tensor(nh, tr, 1.0, nh, ALU.add, ALU.mult).then_inc(s["v1_done"], 1)
                    dve.wait_ge(s["v1_done"], k + 1)
                    for j2 in range(ET):
                        dve.wait_ge(s["x_full"], f0 + 9 + j2)
                        dve.tensor_tensor(nh[:, j2 * L:(j2 + 1) * L], nh[:, j2 * L:(j2 + 1) * L], px[:, (j2 + 1) % 2, :],
                                          ALU.add).then_inc(s["v2_done"], 1)
                elif step == "update":
                    dve.wait_ge(s["d_done"], k + 1)
                    dve.scalar_tensor_tensor(nh, tz, 1.0, nh, ALU.add, ALU.mult).then_inc(s["e_done"], 1)
                    dve.wait_ge(s["e_done"], k + 1)
                    dve.scalar_tensor_tensor(hT[:].rearrange("p a t -> p (a t)"), nh, 0.5, nn, ALU.mult, ALU.add).then_inc(s["h_done"], 1)
                elif step == "final":
                    x2v = x2[:].rearrange("p i e -> p (i e)")
                    if k == 0:
                        if ffn:
                            dve.wait_ge(s["x2_kept"], 1)
                        dve.wait_ge(s["x_full"], 4 + 10 * NI + 1)
                        dve.tensor_tensor(x2v, px[:].rearrange("p a t -> p (a t)"), x1[:].rearrange("p i e -> p (i e)"),
                                          ALU.add).then_inc(s["xs_done"], 1)
                        dve.wait_ge(s["xs_done"], 1)
                        norm_stats("x2", x2)
                    if k == 1:
                        norm_apply("x2", x2, x2)

            def spike(n):
                done = s["early_spike"] if n < EARLY_SPIKES else s["spike"]
                if n == 0:
                    dve.wait_ge(s["unit_read"], 2 * (UPS + TT // 2))
                    dve.tensor_scalar(cnt, y_sb, THRESHOLD, None, ALU.is_gt).then_inc(done, 1)
                    return
                if n != EARLY_SPIKES:
                    dve.wait_ge(done, n if n < EARLY_SPIKES else n - EARLY_SPIKES)
                if n == SPIKE_OPS - 1:
                    dve.scalar_tensor_tensor(mem, cnt, 1.0 / STEPS, x2_old[:].rearrange("p i e -> p (i e)"), ALU.mult,
                                             ALU.add).then_inc(s["out_res"], 1)
                    return
                t, k = divmod(n - 1, 3)
                old = mem if t else y_sb
                if k == 0:
                    ins = dve.scalar_tensor_tensor(acc, old, BETA, y_sb, ALU.mult, ALU.add)
                if k == 1:
                    ins = dve.scalar_tensor_tensor(mem, old, THRESHOLD, acc, ALU.is_gt, ALU.subtract, reverse1=True)
                if k == 2:
                    ins = dve.scalar_tensor_tensor(cnt, mem, THRESHOLD, cnt, ALU.is_gt, ALU.add)
                ins.then_inc(done, 1)

            memv = mem.rearrange("p (i e) -> p i e", e=E)
            accv = acc.rearrange("p (i e) -> p i e", e=E)

            def body(i, mamba, slots, ffn, spikes):
                def filler(position):
                    take(position, slot_step, mamba, slots, ffn, spikes)

                def gate(c):
                    dve.wait_ge(s["zth_ready"], c + 1)
                    dve.scalar_tensor_tensor(sz[:, c], sz[:, c], 1.0, z_banks[c], ALU.add, ALU.mult).then_inc(s["sz_ready"], 1)

                filler("start")
                if mamba:
                    for c0 in (0, 2):
                        for t in range(KC - 1):
                            for c in (c0, c0 + 1):
                                if t:
                                    dve.wait_ge(s["conv_step"], 3 * c0 + 2 * t + c - c0 - 1)
                                dve.scalar_tensor_tensor(u2[:, c], upad[:, c, t:t + L], col("conv_w", c * KC + t), u2[:, c],
                                                         ALU.mult, ALU.add).then_inc(s["conv_step"], 1)
                filler("z")
                if mamba:
                    for c in range(DT):
                        dve.wait_ge(s["uth_ready"], c + 1)
                        dve.scalar_tensor_tensor(u2[:, c], dtu[:, c], 1.0, u2[:, c], ALU.add, ALU.mult).then_inc(s["u_ready"], 1)
                    for c in range(DT):
                        gate(c)
                filler("x")
                if mamba:
                    dve.wait_ge(s["pre_full"], 1)
                    dve.tensor_copy(bcs[:], pb[0:3 * BC, 2, :]).then_inc(s["bc_split"], 1)
                    dve.wait_ge(s["bc_split"], 1)
                    dve.tensor_tensor(bcr, pb[0:3 * BC, 2, :], bcs[:], ALU.subtract).then_inc(s["bc_split"], 1)
                    dve.wait_ge(s["bc_split"], 2)
                    dve.tensor_copy(bcs[BC:2 * BC], bcr[BC:2 * BC]).then_inc(s["bc_split"], 1)
                    dve.tensor_copy(bcs[2 * BC:3 * BC], bcr[2 * BC:3 * BC]).then_inc(s["bc_split"], 1)
                    dve.wait_ge(s["bc_split"], 4)
                    dve.tensor_tensor(bcs[2 * BC:3 * BC], bcr[2 * BC:3 * BC], bcs[2 * BC:3 * BC], ALU.subtract).then_inc(s["bc_split"], 1)

                filler("dt")

                def mul(g):
                    c, b = g // PAIRS, 2 * (g % 2)
                    dve.wait_ge(s["bcb_full"], g + 1)
                    if g % PAIRS == 0:
                        dve.wait_ge(s["dtu_ready"], c + 1)
                    dve.tensor_tensor(pb[:, b:b + 2, :], pb[:, b:b + 2, :], dtu[:, c:c + 1, :].to_broadcast([P, 2, L]),
                                      ALU.mult).then_inc(s["mul_done"], 1)

                def scan(g):
                    b = 2 * (g % 2)
                    dve.wait_ge(s["da_ready"], g + 1)
                    dve.wait_ge(s["mul_done"], g + 1)
                    if g >= HR:
                        dve.wait_ge(s["hsum_done"], g - HR + 1)
                    dve.tensor_tensor_scan(h2[:, g % HR], d_a2[:, g % 2], pb[:, b:b + 2, :].rearrange("p a t -> p (a t)"), 0.0,
                                           ALU.mult, ALU.add).then_inc(s["scan_done"], 1)

                for g in range(SLOTS):
                    if mamba:
                        if g == 0:
                            mul(0)
                        if g < GROUPS:
                            scan(g)
                        if g + 1 < GROUPS:
                            mul(g + 1)
                        if chunk_end(g) is not None:
                            c = chunk_end(g)
                            dve.wait_ge(s["yback_full"], c + 1)
                            dve.scalar_tensor_tensor(yv[:, c], u2[:, c], half_d[:, c:c + 1], pc[:], ALU.mult, ALU.add).then_inc(s["ypost_done"], 1)
                        if g == MERGE_SLOT and not slots:
                            dve.wait_ge(late_weights_in, 16 * len(late_loads))
                            dve.tensor_scalar(w_out[:], w_out[:], 0.5, None, ALU.mult)
                    filler(g)
                filler("end")
                if mamba:
                    dve.wait_ge(s["op_half"], 1)
                    norm_apply("next", xin, xn)
                    dve.wait_ge(s["xres_load"], 16)
                    for i2 in range(TT):
                        dve.wait_ge(s["op_full"], i2 + 1)
                        dve.scalar_tensor_tensor(xres[:, i2], xres[:, i2], 2.0, pb[:, i2, 0:E], ALU.mult, ALU.add).then_inc(s["res_done"], 1)
                    dve.wait_ge(s["res_done"], TT)
                    norm_stats("post", xres)
                filler("post")
                if mamba:
                    norm_apply("post", xres, x1)
                meet(dve, i + 2)

            iterations(dve, body)


def kernel(**inputs):
    import numpy as np
    import concourse.bacc as bacc
    from concourse.bass_utils import run_bass_kernel_spmd

    def rows(a, n):
        a = np.asarray(a).reshape(n, P, -1)
        return a.transpose(1, 0, 2).reshape(P, -1)

    w = {k: np.asarray(v) for k, v in inputs.items()}
    w_x = w["L0_attn_W_x"].T
    cols = np.concatenate([rows(w["L0_attn_conv_w"], DT), rows(w["L0_attn_conv_b"], DT), rows(w["L0_attn_dt_bias"], DT),
                           rows(w["L0_attn_A_log"], DT), rows(w["L0_attn_D"], DT), rows(w["L0_xattn_gru_bih"], 6),
                           rows(w["L0_xattn_gru_bhh"], 6), rows(w["L0_xattn_slot_norm_w"], ET),
                           rows(w["L0_xattn_input_norm_w"], ET), rows(w["L0_attn_ln_g"], ET), rows(w["L0_attn_ln_b"], ET)], axis=1)
    arrays = {
        "x_in": w["x"], "ctx_in": w["ctx_1024"], "cols_in": cols,
        "w_inT_in": w["L0_attn_W_in"].T,
        "w_xT_in": np.concatenate([w_x[:, DTR:]] * 3 + [w_x[:, :DTR]], axis=1),
        "w_dtT_in": w["L0_attn_W_dt"].T, "w_outT_in": w["L0_attn_W_out"].T,
        "wq_in": w["L0_xattn_Wq"], "wk_in": w["L0_xattn_Wk"], "wv_in": w["L0_xattn_Wv"],
        "wihT_in": w["L0_xattn_gru_wih"].T, "whhT_in": w["L0_xattn_gru_whh"].T,
        "w_fcT_in": w["L0_ffn_W_fc"].T, "w_prT_in": w["L0_ffn_W_proj"].T,
    }
    arrays = {k: np.ascontiguousarray(v) for k, v in arrays.items()}
    nc = bacc.Bacc("TRN2", target_bir_lowering=False, num_devices=1)
    args = [nc.dram_tensor(k, a.shape, F32, kind="ExternalInput").ap() for k, a in arrays.items()]
    out = nc.dram_tensor("x_out", (BATCH, L, E), F32, kind="ExternalOutput").ap()
    decoder_layer(nc, *args, out)
    r = run_bass_kernel_spmd(nc, [arrays], core_ids=[0])
    return r.results[0]["x_out"]
```
